# Optimizing a Trainium2 kernel written in Bass

```python
import numpy as np
import jax
import jax.numpy as jnp

def _softmax(x, axis=-1):
    return jax.nn.softmax(x, axis=axis)

def _gelu(x):
    return jax.nn.gelu(x, approximate=True)

def _silu(x):
    return jax.nn.silu(x)

def _sigmoid(x):
    return jax.nn.sigmoid(x)

def _layernorm(x, axis=-1, eps=1e-05):
    m = jnp.mean(x, axis=axis, keepdims=True)
    v = jnp.var(x, axis=axis, keepdims=True)
    return (x - m) / jnp.sqrt(v + eps)

def _scatter_add(tgt, idx, src, axis=0):
    return tgt.at[idx].add(src)

def _segment_sum(src, seg, n):
    return jax.ops.segment_sum(src, seg, n)
kernel_name = 'mk_adaln_d2_jaxref_r8_3722af'

def setup_inputs(seed: int=0):
    np.random.seed(seed)
    _w = jnp.asarray

    def _L0_attn_setup():
        import jax, jax.numpy as jnp
        import numpy as np
        import math
        D_MODEL = 128
        N_HEADS = 16
        LATENT = 32
        key = jax.random.key(seed)
        ks = jax.random.split(key, 9)
        B, T, C, L = (2, 256, D_MODEL, LATENT)
        s = 0.02
        return {'x': jax.random.normal(ks[0], (B, T, C), dtype=jnp.float32), 'Wq': jax.random.normal(ks[1], (C, C), dtype=jnp.float32) * s, 'bq': jnp.zeros((C,), dtype=jnp.float32), 'Wkd': jax.random.normal(ks[2], (C, 2 * L), dtype=jnp.float32) * s, 'bkd': jnp.zeros((2 * L,), dtype=jnp.float32), 'Wku': jax.random.normal(ks[3], (L, 2 * C), dtype=jnp.float32) * s, 'bku': jnp.zeros((2 * C,), dtype=jnp.float32), 'Wo': jax.random.normal(ks[4], (C, C), dtype=jnp.float32) * s, 'bo': jnp.zeros((C,), dtype=jnp.float32)}
    _L0_attn_in = _L0_attn_setup()

    def _L0_ffn_setup():
        import jax, jax.numpy as jnp
        import numpy as np
        D_MODEL = 128
        D_FF = 512
        N_EXPERTS = 8
        TOP_K = 2

        def _ffn(x, w1, b1, w2, b2):
            h = jax.nn.gelu(x @ w1.T + b1)
            return h @ w2.T + b2
        key = jax.random.key(seed)
        ks = jax.random.split(key, 12)
        s = 0.02
        x = jax.random.normal(ks[0], (4, 256, D_MODEL), dtype=jnp.float32)
        shared_w1 = jax.random.normal(ks[1], (D_FF, D_MODEL), dtype=jnp.float32) * s
        shared_b1 = jnp.zeros((D_FF,), dtype=jnp.float32)
        shared_w2 = jax.random.normal(ks[2], (D_MODEL, D_FF), dtype=jnp.float32) * s
        shared_b2 = jnp.zeros((D_MODEL,), dtype=jnp.float32)
        router_w = jax.random.normal(ks[3], (N_EXPERTS, D_MODEL), dtype=jnp.float32) * s
        router_b = jnp.zeros((N_EXPERTS,), dtype=jnp.float32)
        spec_w1 = jax.random.normal(ks[4], (N_EXPERTS, D_FF, D_MODEL), dtype=jnp.float32) * s
        spec_b1 = jnp.zeros((N_EXPERTS, D_FF), dtype=jnp.float32)
        spec_w2 = jax.random.normal(ks[5], (N_EXPERTS, D_MODEL, D_FF), dtype=jnp.float32) * s
        spec_b2 = jnp.zeros((N_EXPERTS, D_MODEL), dtype=jnp.float32)
        return dict(x=x, shared_w1=shared_w1, shared_b1=shared_b1, shared_w2=shared_w2, shared_b2=shared_b2, router_w=router_w, router_b=router_b, spec_w1=spec_w1, spec_b1=spec_b1, spec_w2=spec_w2, spec_b2=spec_b2)
    _L0_ffn_in = _L0_ffn_setup()
    _L0_c = _w((lambda *s: np.random.randn(*s).astype(np.float32) * 0.05)(8, 128))
    _L0_wmod = _w((lambda *s: np.random.randn(*s).astype(np.float32) * 0.05)(128, 6 * 128) * 128 ** (-0.5))

    def _L1_attn_setup():
        import jax, jax.numpy as jnp
        import numpy as np
        D = 128
        B = 16
        L = 256

        def _lin_init(key, din, dout):
            kw, kb = jax.random.split(key)
            s = 1.0 / np.sqrt(din)
            w = jax.random.uniform(kw, (dout, din), minval=-s, maxval=s, dtype=jnp.float32)
            b = jax.random.uniform(kb, (dout,), minval=-s, maxval=s, dtype=jnp.float32)
            return (w, b)

        def _rms_norm(x, w, eps=1e-06):
            x32 = x.astype(jnp.float32)
            y = x32 * jax.lax.rsqrt(jnp.mean(x32 * x32, axis=-1, keepdims=True) + eps)
            return y.astype(x.dtype) * w
        key = jax.random.key(seed)
        ks = jax.random.split(key, 9)
        fc_w, fc_b = _lin_init(ks[0], D, D)
        fc_r_w, fc_r_b = _lin_init(ks[1], D, D)
        fc_i_w, fc_i_b = _lin_init(ks[2], D, D)
        fc_gate_w, fc_gate_b = _lin_init(ks[3], D, D)
        mlp_gate_w, mlp_gate_b = _lin_init(ks[4], D, 3 * D)
        mlp_fc_w, mlp_fc_b = _lin_init(ks[5], D, 3 * D)
        out_w, out_b = _lin_init(ks[6], 3 * D, D)
        alpha = jax.random.uniform(ks[7], (1, 1, D), dtype=jnp.float32) * (0.999 - 0.9) + 0.9
        hidden_states = jax.random.normal(ks[8], (B, L, D), dtype=jnp.float32)
        return dict(hidden_states=hidden_states, alpha=alpha, fc_w=fc_w, fc_b=fc_b, fc_r_w=fc_r_w, fc_r_b=fc_r_b, fc_i_w=fc_i_w, fc_i_b=fc_i_b, fc_gate_w=fc_gate_w, fc_gate_b=fc_gate_b, norm_w=jnp.ones((D,), jnp.float32), norm2_w=jnp.ones((D,), jnp.float32), mlp_gate_w=mlp_gate_w, mlp_gate_b=mlp_gate_b, mlp_fc_w=mlp_fc_w, mlp_fc_b=mlp_fc_b, out_w=out_w, out_b=out_b)
    _L1_attn_in = _L1_attn_setup()

    def _L1_ffn_setup():
        import jax, jax.numpy as jnp
        import numpy as np
        B, S, D, F, E, K = (4, 256, 128, 256, 8, 2)
        key = jax.random.key(seed)
        k0, k1, k2, k3, k4 = jax.random.split(key, 5)
        sD = 1.0 / np.sqrt(D).astype(np.float32)
        sF = 1.0 / np.sqrt(F).astype(np.float32)
        return {'hidden_states': jax.random.normal(k0, (B, S, D), jnp.float32), 'Wg': jax.random.normal(k1, (D, E), jnp.float32) * sD, 'W1': jax.random.normal(k2, (E, D, F), jnp.float32) * sD, 'W3': jax.random.normal(k3, (E, D, F), jnp.float32) * sD, 'W2': jax.random.normal(k4, (E, F, D), jnp.float32) * sF}
    _L1_ffn_in = _L1_ffn_setup()
    _L1_c = _w((lambda *s: np.random.randn(*s).astype(np.float32) * 0.05)(8, 128))
    _L1_wmod = _w((lambda *s: np.random.randn(*s).astype(np.float32) * 0.05)(128, 6 * 128) * 128 ** (-0.5))
    _d = {'L0_attn_x': _L0_attn_in['x'], 'L0_attn_Wq': _L0_attn_in['Wq'], 'L0_attn_bq': _L0_attn_in['bq'], 'L0_attn_Wkd': _L0_attn_in['Wkd'], 'L0_attn_bkd': _L0_attn_in['bkd'], 'L0_attn_Wku': _L0_attn_in['Wku'], 'L0_attn_bku': _L0_attn_in['bku'], 'L0_attn_Wo': _L0_attn_in['Wo'], 'L0_attn_bo': _L0_attn_in['bo'], 'L0_ffn_shared_w1': _L0_ffn_in['shared_w1'], 'L0_ffn_shared_b1': _L0_ffn_in['shared_b1'], 'L0_ffn_shared_w2': _L0_ffn_in['shared_w2'], 'L0_ffn_shared_b2': _L0_ffn_in['shared_b2'], 'L0_ffn_router_w': _L0_ffn_in['router_w'], 'L0_ffn_router_b': _L0_ffn_in['router_b'], 'L0_ffn_spec_w1': _L0_ffn_in['spec_w1'], 'L0_ffn_spec_b1': _L0_ffn_in['spec_b1'], 'L0_ffn_spec_w2': _L0_ffn_in['spec_w2'], 'L0_ffn_spec_b2': _L0_ffn_in['spec_b2'], 'L0_c': _L0_c, 'L0_wmod': _L0_wmod, 'L1_attn_alpha': _L1_attn_in['alpha'], 'L1_attn_fc_w': _L1_attn_in['fc_w'], 'L1_attn_fc_b': _L1_attn_in['fc_b'], 'L1_attn_fc_r_w': _L1_attn_in['fc_r_w'], 'L1_attn_fc_r_b': _L1_attn_in['fc_r_b'], 'L1_attn_fc_i_w': _L1_attn_in['fc_i_w'], 'L1_attn_fc_i_b': _L1_attn_in['fc_i_b'], 'L1_attn_fc_gate_w': _L1_attn_in['fc_gate_w'], 'L1_attn_fc_gate_b': _L1_attn_in['fc_gate_b'], 'L1_attn_norm_w': _L1_attn_in['norm_w'], 'L1_attn_norm2_w': _L1_attn_in['norm2_w'], 'L1_attn_mlp_gate_w': _L1_attn_in['mlp_gate_w'], 'L1_attn_mlp_gate_b': _L1_attn_in['mlp_gate_b'], 'L1_attn_mlp_fc_w': _L1_attn_in['mlp_fc_w'], 'L1_attn_mlp_fc_b': _L1_attn_in['mlp_fc_b'], 'L1_attn_out_w': _L1_attn_in['out_w'], 'L1_attn_out_b': _L1_attn_in['out_b'], 'L1_ffn_Wg': _L1_ffn_in['Wg'], 'L1_ffn_W1': _L1_ffn_in['W1'], 'L1_ffn_W3': _L1_ffn_in['W3'], 'L1_ffn_W2': _L1_ffn_in['W2'], 'L1_c': _L1_c, 'L1_wmod': _L1_wmod}
    _x0 = _d['L0_attn_x']
    _d['L0_attn_x'] = jax.random.normal(jax.random.fold_in(jax.random.key(seed), 1), (8, 256, 128), dtype=_x0.dtype)
    del _x0
    return _d

def reference(L0_attn_x, L0_attn_Wq, L0_attn_bq, L0_attn_Wkd, L0_attn_bkd, L0_attn_Wku, L0_attn_bku, L0_attn_Wo, L0_attn_bo, L0_ffn_shared_w1, L0_ffn_shared_b1, L0_ffn_shared_w2, L0_ffn_shared_b2, L0_ffn_router_w, L0_ffn_router_b, L0_ffn_spec_w1, L0_ffn_spec_b1, L0_ffn_spec_w2, L0_ffn_spec_b2, L0_c, L0_wmod, L1_attn_alpha, L1_attn_fc_w, L1_attn_fc_b, L1_attn_fc_r_w, L1_attn_fc_r_b, L1_attn_fc_i_w, L1_attn_fc_i_b, L1_attn_fc_gate_w, L1_attn_fc_gate_b, L1_attn_norm_w, L1_attn_norm2_w, L1_attn_mlp_gate_w, L1_attn_mlp_gate_b, L1_attn_mlp_fc_w, L1_attn_mlp_fc_b, L1_attn_out_w, L1_attn_out_b, L1_ffn_Wg, L1_ffn_W1, L1_ffn_W3, L1_ffn_W2, L1_c, L1_wmod):

    def _L0_attn_ref(x, Wq, bq, Wkd, bkd, Wku, bku, Wo, bo):
        import jax, jax.numpy as jnp
        import numpy as np
        import math
        D_MODEL = 128
        N_HEADS = 16
        LATENT = 32
        B, T, C = x.shape
        H = N_HEADS
        D = C // H
        L = LATENT
        q = (x @ Wq + bq).reshape(B, T, H, D)
        kv_latent = jax.nn.gelu(x @ Wkd + bkd, approximate=False)
        lat = kv_latent[..., :L] + kv_latent[..., L:]
        kv = lat @ Wku + bku
        k = kv[..., :C].reshape(B, T, H, D)
        v = kv[..., C:].reshape(B, T, H, D)
        scale = 1.0 / math.sqrt(D)
        attn = jnp.einsum('bqhd,bkhd->bhqk', q, k) * scale
        causal = jnp.tril(jnp.ones((T, T), dtype=bool))
        attn = jnp.where(causal, attn, -jnp.inf)
        attn = jax.nn.softmax(attn, axis=-1)
        out = jnp.einsum('bhqk,bkhd->bqhd', attn, v).reshape(B, T, C)
        return out @ Wo + bo

    def _L0_ffn_ref(x, shared_w1, shared_b1, shared_w2, shared_b2, router_w, router_b, spec_w1, spec_b1, spec_w2, spec_b2):
        import jax, jax.numpy as jnp
        import numpy as np
        D_MODEL = 128
        D_FF = 512
        N_EXPERTS = 8
        TOP_K = 2

        def _ffn(x, w1, b1, w2, b2):
            h = jax.nn.gelu(x @ w1.T + b1)
            return h @ w2.T + b2
        B, T, D = x.shape
        xf = x.reshape(-1, D)
        U = xf.shape[0]
        logits = xf @ router_w.T + router_b
        routing = jax.nn.softmax(logits, axis=-1)
        sel_w, sel_idx = jax.lax.top_k(routing, TOP_K)
        sel_w = sel_w / sel_w.sum(axis=-1, keepdims=True)
        comb = jnp.zeros_like(routing).at[jnp.arange(U)[:, None], sel_idx].set(sel_w)
        shared_out = _ffn(xf, shared_w1, shared_b1, shared_w2, shared_b2)

        def body(acc, params):
            w1, b1, w2, b2, we = params
            return (acc + we[:, None] * _ffn(xf, w1, b1, w2, b2), None)
        acc0 = jnp.zeros_like(shared_out)
        acc, _ = jax.lax.scan(body, acc0, (spec_w1, spec_b1, spec_w2, spec_b2, comb.T))
        return (shared_out + acc).reshape(B, T, D)

    def _L1_attn_ref(hidden_states, alpha, fc_w, fc_b, fc_r_w, fc_r_b, fc_i_w, fc_i_b, fc_gate_w, fc_gate_b, norm_w, norm2_w, mlp_gate_w, mlp_gate_b, mlp_fc_w, mlp_fc_b, out_w, out_b):
        import jax, jax.numpy as jnp
        import numpy as np
        D = 128
        B = 16
        L = 256

        def _lin_init(key, din, dout):
            kw, kb = jax.random.split(key)
            s = 1.0 / np.sqrt(din)
            w = jax.random.uniform(kw, (dout, din), minval=-s, maxval=s, dtype=jnp.float32)
            b = jax.random.uniform(kb, (dout,), minval=-s, maxval=s, dtype=jnp.float32)
            return (w, b)

        def _rms_norm(x, w, eps=1e-06):
            x32 = x.astype(jnp.float32)
            y = x32 * jax.lax.rsqrt(jnp.mean(x32 * x32, axis=-1, keepdims=True) + eps)
            return y.astype(x.dtype) * w
        residual = hidden_states
        h = _rms_norm(hidden_states, norm_w)
        gate = jax.nn.gelu(h @ fc_gate_w.T + fc_gate_b, approximate=False)
        hs = h @ fc_w.T + fc_b
        r = jax.nn.sigmoid(h @ fc_r_w.T + fc_r_b)
        i = jax.nn.sigmoid(h @ fc_i_w.T + fc_i_b)
        a = jnp.exp(-8.0 * jax.nn.softplus(alpha) * r)
        s = jnp.sqrt(1.0 - a * a) * hs * i

        def step(carry, xs):
            a_t, s_t = xs
            o = a_t * carry + s_t
            return (o, o)
        a_l = jnp.swapaxes(a, 0, 1)
        s_l = jnp.swapaxes(s, 0, 1)
        _, out_l = jax.lax.scan(step, jnp.zeros_like(s_l[0]), (a_l, s_l))
        out = jnp.swapaxes(out_l, 0, 1)
        hs2 = out * gate + residual
        h2 = _rms_norm(hs2, norm2_w)
        g2 = jax.nn.gelu(h2 @ mlp_gate_w.T + mlp_gate_b, approximate=False)
        f2 = h2 @ mlp_fc_w.T + mlp_fc_b
        return f2 * g2 @ out_w.T + out_b + hs2

    def _L1_ffn_ref(hidden_states, Wg, W1, W3, W2):
        import jax, jax.numpy as jnp
        import numpy as np
        B, S, D, F, E, K = (4, 256, 128, 256, 8, 2)
        b, s, d = hidden_states.shape
        e = Wg.shape[1]
        x = hidden_states.reshape(-1, d)
        t = x.shape[0]
        gates = jax.nn.softmax(x @ Wg, axis=-1)
        top_g, top_i = jax.lax.top_k(gates, K)
        top_g = top_g / top_g.sum(axis=-1, keepdims=True)
        w = jnp.zeros((t, e), x.dtype).at[jnp.arange(t)[:, None], top_i].add(top_g)
        gate_h = jax.nn.silu(jnp.einsum('td,edf->etf', x, W1))
        up = jnp.einsum('td,edf->etf', x, W3)
        y = jnp.einsum('etf,efd->etd', gate_h * up, W2)
        out = jnp.einsum('te,etd->td', w, y)
        return out.reshape(b, s, d)
    x = L0_attn_x
    mod = (_silu(L0_c) @ L0_wmod).reshape(L0_c.shape[0], 6, 1, -1)
    sa, ca, ga, sb, cb, gb = (mod[:, 0], mod[:, 1], mod[:, 2], mod[:, 3], mod[:, 4], mod[:, 5])
    ga = (2 * (ga >= 0) - 1) * jnp.maximum(jnp.abs(ga), 0.25)
    gb = (2 * (gb >= 0) - 1) * jnp.maximum(jnp.abs(gb), 0.25)
    h = _layernorm(x, axis=-1) * (1 + ca) + sa
    x = x + ga * _L0_attn_ref(h, L0_attn_Wq, L0_attn_bq, L0_attn_Wkd, L0_attn_bkd, L0_attn_Wku, L0_attn_bku, L0_attn_Wo, L0_attn_bo)
    h = _layernorm(x, axis=-1) * (1 + cb) + sb
    x = x + gb * _L0_ffn_ref(h, L0_ffn_shared_w1, L0_ffn_shared_b1, L0_ffn_shared_w2, L0_ffn_shared_b2, L0_ffn_router_w, L0_ffn_router_b, L0_ffn_spec_w1, L0_ffn_spec_b1, L0_ffn_spec_w2, L0_ffn_spec_b2)
    mod = (_silu(L1_c) @ L1_wmod).reshape(L1_c.shape[0], 6, 1, -1)
    sa, ca, ga, sb, cb, gb = (mod[:, 0], mod[:, 1], mod[:, 2], mod[:, 3], mod[:, 4], mod[:, 5])
    ga = (2 * (ga >= 0) - 1) * jnp.maximum(jnp.abs(ga), 0.25)
    gb = (2 * (gb >= 0) - 1) * jnp.maximum(jnp.abs(gb), 0.25)
    h = _layernorm(x, axis=-1) * (1 + ca) + sa
    x = x + ga * _L1_attn_ref(h, L1_attn_alpha, L1_attn_fc_w, L1_attn_fc_b, L1_attn_fc_r_w, L1_attn_fc_r_b, L1_attn_fc_i_w, L1_attn_fc_i_b, L1_attn_fc_gate_w, L1_attn_fc_gate_b, L1_attn_norm_w, L1_attn_norm2_w, L1_attn_mlp_gate_w, L1_attn_mlp_gate_b, L1_attn_mlp_fc_w, L1_attn_mlp_fc_b, L1_attn_out_w, L1_attn_out_b)
    h = _layernorm(x, axis=-1) * (1 + cb) + sb
    x = x + gb * _L1_ffn_ref(h, L1_ffn_Wg, L1_ffn_W1, L1_ffn_W3, L1_ffn_W2)
    return x

_drawn_inputs = setup_inputs


def setup_inputs(seed=0):
    import zlib

    import numpy as np

    out = dict(_drawn_inputs(seed))
    spreads = {'L0_attn_bq': (0.0, 0.8),
     'L0_attn_bkd': (0.0, 0.8),
     'L0_attn_bku': (0.0, 0.8),
     'L0_attn_bo': (0.0, 0.279),
     'L0_ffn_shared_b1': (0.0, 0.8),
     'L0_ffn_shared_b2': (0.0, 0.276),
     'L0_ffn_router_b': (0.0, 0.557),
     'L0_ffn_spec_b1': (0.0, 0.8),
     'L0_ffn_spec_b2': (0.0, 0.365),
     'L1_attn_norm_w': (1.0, 0.6),
     'L1_attn_norm2_w': (1.0, 0.6)}
    factors = {'L0_attn_Wq': 8.0,
     'L0_attn_Wkd': 8.0,
     'L0_attn_Wku': 8.0,
     'L0_attn_Wo': 6.822,
     'L0_ffn_shared_w1': 3.398,
     'L0_ffn_shared_w2': 3.151,
     'L0_ffn_router_w': 2.843,
     'L0_ffn_spec_w1': 4.985,
     'L0_ffn_spec_w2': 4.568,
     'L1_attn_alpha': 64.0,
     'L1_attn_fc_b': 8.0,
     'L1_attn_fc_r_w': 8.0,
     'L1_attn_fc_r_b': 64.0,
     'L1_attn_fc_i_w': 5.785,
     'L1_attn_fc_i_b': 57.316,
     'L1_attn_fc_gate_b': 8.0,
     'L1_attn_mlp_gate_b': 8.0,
     'L1_attn_mlp_fc_b': 8.0,
     'L1_attn_out_b': 6.45}
    for name, (base, spread) in spreads.items():
        noise = np.random.default_rng([zlib.crc32(name.encode()), seed]).standard_normal(out[name].shape)
        drawn = base * np.exp(spread * noise) if base else spread * noise
        out[name] = jnp.asarray(drawn.astype(out[name].dtype))
    for name, factor in factors.items():
        out[name] = (out[name] * factor).astype(out[name].dtype)
    return out
```

```python
import concourse.bass as bass
from concourse import mybir
from contextlib import ExitStack

TOK, D, BATCHES, SEQ = 2048, 128, 8, 256
BLK, NBLK = 512, 4
HEADS, HD, GROUPS = 16, 8, 4
UNITS = BATCHES * GROUPS
E0, F0 = 9, 512
E1, F1 = 8, 256
SCALE = HD ** -0.5
MASKED = -1e30

VECS = dict(bo=1, bq=4, bk=4, q_sign=1, q_keep=1, k_sign=1, k_keep=1, b1=4 * E0, pb=4, gb=3, fb=3,
            outb=1, alpha=1, norm=1, norm2=1, bkd=1, c=16, prio=8)
MATS = dict(wkd=64, wq=512, wo=512, router=8, wg=8, l1=4 * 128 + 3 * 384)


def columns(widths):
    at, out = 0, {}
    for name, width in widths.items():
        out[name] = at
        at += width
    return out, at


VAT, VN = columns(VECS)
MAT_AT, MN = columns(MATS)


def build(nc, xT, wmod, vecs, mats, kmats, rows, b2, w0, w1, comb0, comb1, outT):
    f32, r32, bf16 = mybir.dt.float32, mybir.dt.float32r, mybir.dt.bfloat16
    ALU, ACT, AX = mybir.AluOpType, mybir.ActivationFunctionType, mybir.AxisListType
    ctx = ExitStack()
    with ctx:
        def sb(name, shape, dt=f32):
            return ctx.enter_context(nc.sbuf_tensor(name, shape, dt))

        def sem(name):
            return ctx.enter_context(nc.semaphore(name))

        def f(ap):
            return ap.bitcast(f32)

        def blk(tile, t, n=BLK):
            return tile[:, t * n:(t + 1) * n]

        X = sb("X", [128, TOK])
        HN = sb("HN", [128, TOK])
        HH = sb("HH", [128, TOK], r32)
        HL = sb("HL", [128, TOK], r32)
        XC = sb("XC", [128, TOK])
        STAT = sb("STAT", [128, TOK])
        AR = sb("AR", [128, 17408])
        RA = sb("RA", [128, 8192], r32)
        WS = sb("WS", [128, 1024])
        WH = sb("WH", [128, 2, 1024], r32)
        WL = sb("WL", [128, 2, 1024], r32)
        V = sb("V", [128, VN])
        M = sb("M", [128, MN])
        LH = sb("LH", [128, MATS["l1"]], r32)
        LL = sb("LL", [128, MATS["l1"]], r32)
        KM = sb("KM", [64, 640])
        ROWS = sb("ROWS", [128, 136])
        B2 = sb("B2", [E0, 128])
        MOD = sb("MOD", [128, 2, 6, 8])
        MC = sb("MC", [128, 2, 2, 8])
        GS = sb("GS", [128, 2, 2, 8])
        GA = sb("GA", [128, 2, 2, 8])
        MG = sb("MG", [128, 2, 2, 8])
        BI = sb("BI", [128, 2, 4])
        SC = sb("SC", [128, 16])
        CON = sb("CON", [128, 4])
        OND = sb("OND", [128, 128])
        IDF = sb("IDF", [128, 128])
        IDB = sb("IDB", [128, 128], bf16)
        MKQ = sb("MKQ", [128, 128], bf16)
        MKK = sb("MKK", [128, 128], bf16)
        SP = sb("SP", [128, 4])
        PS = ctx.enter_context(nc.psum_tensor("PS", [128, 8, 512], f32))

        def vec(name, i=0):
            return V[:, VAT[name] + i:VAT[name] + i + 1]

        def mat(name, i=0, n=128):
            return M[:, MAT_AT[name] + i * n:MAT_AT[name] + (i + 1) * n]

        WMOD = AR[:, 0:1536]
        ON = AR[:, 0:8192].rearrange("p (g n) -> p g n", g=4)
        LAT = AR[0:64, 8192:10240]
        VALL = AR[:, 10240:12288].rearrange("p (i c) -> p i c", i=16)
        PR = AR[:, 12288:15360].rearrange("p (r j n) -> p r j n", r=2, j=4)
        VX = (HH, HL)
        PL = (WH, WL)
        QX = RA[:, 0:1024].rearrange("p (g n) -> p g n", g=4)
        KX = RA[:, 1024:2048].rearrange("p (g n) -> p g n", g=4)
        QM = RA[:, 2048:2560].rearrange("p (r n) -> p r n", r=2)
        QR = RA[:, 2560:2816]
        KR = RA[:, 2816:3072]
        NMH = RA[:, 3072:3080]
        PH = RA[:, 3080:6152].rearrange("p (r j n) -> p r j n", r=2, j=4)
        QT = sb("QT", [128, 256])
        KT = sb("KT", [128, 256])
        NM = sb("NM", [128, 8])
        MP = sb("MP", [128, 2, 128])
        OT = sb("OT", [128, 2, 256])
        SU = sb("SU", [128, 2, 256])
        G = AR[:, 0:2048].rearrange("p (c n) -> p c n", c=4)
        SG = AR[:, 2048:3072].rearrange("p (c n) -> p c n", c=2)
        YW = AR[:, 3072:4096].rearrange("p (r n) -> p r n", r=2)
        ACC = AR[:, 4096:6144]
        WB = AR[:, 6144:10240].rearrange("p (r n) -> p r n", r=2)
        CT = AR[:, 10240:12288]
        GH = RA[:, 0:4096].rearrange("p (r c n) -> p r c n", r=2, c=4)
        GL = RA[:, 4096:8192].rearrange("p (r c n) -> p r c n", r=2, c=4)
        R_, I_, GATE, HS, A_, SA = (AR[:, 2048 * i:2048 * (i + 1)] for i in range(6))
        H2 = AR[:, 12288:14336]
        GG = AR[:, 14336:15872].rearrange("p (c n) -> p c n", c=3)
        PF = AR[:, 15872:17408].rearrange("p (c n) -> p c n", c=3)
        RT = {n: AR[:, 12288 + 128 * i:12416 + 128 * i].rearrange("p (i e) -> p i e", e=8)
              for i, n in enumerate(("lg", "e", "k1", "k2", "e2", "w"))}
        RM = {n: sb("RM_" + n, [128, 16]) for n in ("m", "m1", "km1", "m2", "km2", "den")}
        COMB = sb("COMB", [128, 16, E0])

        in_x, in_vec, in_mod, in_mats, in_k, in_rows = map(
            sem, ("in_x", "in_vec", "in_mod", "in_mats", "in_k", "in_rows"))
        const_done, ident_done, silu_done, mod_psum, mod_done, gate_done, sp_done = map(
            sem, ("const_done", "ident_done", "silu_done", "mod_psum", "mod_done", "gate_done", "sp_done"))
        mean_done, cen_done, sq_done, var_done, lnv_done, rstd_done, nrm_done, hn_done, hh_done, hl_done = map(
            sem, ("mean_done", "cen_done", "sq_done", "var_done", "lnv_done", "rstd_done", "nrm_done",
                  "hn_done", "hh_done", "hl_done"))
        x_upd, y_scaled = sem("x_upd"), sem("y_scaled")
        out_done = sem("out_done")
        kd_done, lat_done, v_psum, vall_done, ones_done = map(
            sem, ("kd_done", "lat_done", "v_psum", "vall_done", "ones_done"))
        (proj_done, qk_evac, qx_ready, s_done, max_done, nmh_done, mp_ready, mt_done, qm_ready, st_done,
         exp_done, pv_done, ot_done, su_done, ls_done, rsx_done, on_done, vx_ready, wo_done) = map(
            sem, ("proj_done", "qk_evac", "qx_ready", "s_done", "max_done", "nmh_done", "mp_ready",
                  "mt_done", "qm_ready", "st_done", "exp_done", "pv_done", "ot_done", "su_done",
                  "ls_done", "rsx_done", "on_done", "vx_ready", "wo_done"))
        hi_done, lower_done = sem("hi_done"), sem("lower_done")
        l1_split = sem("l1_split")
        bias_done = sem("bias_done")
        p1_psum, p1_done, a_done, sa_done, hsi_done, sqrt_done, s_ready, scan_done, hs2_mul, hs2_done = map(
            sem, ("p1_psum", "p1_done", "a_done", "sa_done", "hsi_done", "sqrt_done", "s_ready", "scan_done",
                  "hs2_mul", "hs2_done"))
        mlp_psum, gg_done, pf_done, ph_done, pl_done, z_psum, z_done = map(
            sem, ("mlp_psum", "gg_done", "pf_done", "ph_done", "pl_done", "z_psum", "z_done"))

        def moe_sems(n):
            names = ("logits", "lg", "exps", "rstep", "comb", "combT", "ct", "stored", "b2_psum", "acc_init",
                     "w_in", "split", "wb_in0", "wb_in1", "h", "act", "prod", "gh", "lo", "y", "ymul", "acc")
            return {k: sem(f"moe{n}_{k}") for k in names}

        moe = [moe_sems(0), moe_sems(1)]
        block = ctx.enter_context(nc.Block())

        def values_of(kt, a, b):
            return VX[kt][:, :].rearrange("p (h c) -> p h c", c=128)[:, :, 96 + a:96 + b]

        def lower_of(n0, h):
            return PL[n0 % 2][:, :, :].rearrange("p r n -> p (r n)")[:, 768 * h:768 * h + 768]\
                .rearrange("p (j n) -> p j n", j=2)

        def centred(k):
            return {0: 0, 1: 1, 2: 2, 5: 3}[k]

        def split_at(k):
            return {1: 0, 3: 1, 4: 2, 5: 3}[k]

        @block.sync
        def _(sp):
            sp.dma_start(V[:, :], vecs).then_inc(in_vec, 16)
            sp.dma_start(WMOD, wmod).then_inc(in_mod, 16)
            for t in range(NBLK):
                sp.dma_start(blk(X, t), blk(xT, t)).then_inc(in_x, 16)
            sp.dma_start(KM[:, :], kmats).then_inc(in_k, 16)
            sp.dma_start(M[:, :], mats).then_inc(in_mats, 16)
            sp.dma_start(ROWS[:, :], rows).then_inc(in_rows, 16)
            sp.dma_start(B2[:, :], b2).then_inc(in_rows, 16)

            for n, (w, comb, ne, width) in enumerate(((w0, comb0, E0, 1024), (w1, comb1, E1, 768))):
                s = moe[n]

                for e in range(2):
                    if e == 1:
                        sp.wait_ge(s["split"], 2)
                    elif n == 1:
                        sp.wait_ge(moe[0]["split"], 2 * E0)
                    sp.dma_start(WS[:, 0:width], w[e, :, :]).then_inc(s["w_in"], 16)
                sp.wait_ge(s["ct"], 4)
                sp.dma_start(comb, CT[0:ne, :]).then_inc(s["stored"], 16)
                sp.wait_ge(s["stored"], 16)
                for e in range(2):
                    sp.dma_start(WB[:, e, :], comb[e:e + 1, :].to_broadcast([128, TOK])).then_inc(s[f"wb_in{e}"], 16)

                def later(e, slot):
                    sp.wait_ge(s["split"], 2 * e)
                    sp.dma_start(WS[:, 0:width], w[bass.ds(e, 1), :, :].rearrange("a p n -> p (a n)")).then_inc(s["w_in"], 16)
                    sp.wait_ge(s["ymul"], 4 * e - 4)
                    sp.dma_start(WB[:, slot, :], comb[bass.ds(e, 1), :].to_broadcast([128, TOK])).then_inc(s[f"wb_in{slot}"], 16)

                with sp.Fori(0, 3) as it:
                    for u in range(2):
                        later(2 * it + 2 + u, u)
                if ne == 9:
                    later(8, 0)

            for t in range(NBLK):
                sp.wait_ge(x_upd, 4 * 3 + t + 1)
                sp.dma_start(blk(outT, t), blk(X, t)).then_inc(out_done, 16)
            sp.wait_ge(out_done, 16 * NBLK)

        @block.gpsimd
        def _(gp):
            gp.memset(CON[:, 0:1], 1e-5).then_inc(const_done, 1)
            gp.memset(CON[:, 1:2], 1e-6).then_inc(const_done, 1)
            gp.memset(CON[:, 2:3], 1.0).then_inc(const_done, 1)
            gp.memset(OND[:, :], 1.0 / D).then_inc(const_done, 1)
            for m in (IDF, IDB, MKQ, MKK, MP):
                gp.memset(m[:], 0.0).then_inc(ident_done, 1)
            gp.wait_ge(ident_done, 5)
            for m in (IDF, IDB):
                gp.affine_select(out=m[:, :], in_=m[:, :], compare_op=ALU.not_equal, fill=1.0, base=0,
                                 pattern=[[-1, 128]], channel_multiplier=1).then_inc(ident_done, 1)
            gp.affine_select(out=MKQ[:, :], in_=MKQ[:, :], compare_op=ALU.is_ge, fill=MASKED, base=0,
                             pattern=[[-1, 128]], channel_multiplier=1).then_inc(ident_done, 1)
            gp.affine_select(out=MKK[:, :], in_=MKK[:, :], compare_op=ALU.is_ge, fill=MASKED, base=0,
                             pattern=[[1, 128]], channel_multiplier=-1).then_inc(ident_done, 1)
            for kt in range(2):
                gp.memset(f(VX[kt][:, :]), 0.0).then_inc(ones_done, 1)
            gp.wait_ge(ones_done, 2)
            for kt in range(2):
                gp.memset(f(values_of(kt, 16, 24)), 1.0).then_inc(ones_done, 1)
            gp.wait_ge(in_mats, 16)
            lm = M[:, MAT_AT["l1"]:MAT_AT["l1"] + MATS["l1"]]
            gp.tensor_scalar(LH[:, :], lm, 1.0, 0.0, ALU.mult, ALU.add).then_inc(l1_split, 1)
            gp.wait_ge(l1_split, 1)
            gp.tensor_tensor(out=LL[:, :], in0=lm, in1=f(LH[:, :]), op=ALU.subtract).then_inc(l1_split, 1)

            def split_weights(n, e, slot, width):
                s = moe[n]
                gp.tensor_scalar(WH[:, slot, 0:width], WS[:, 0:width], 1.0, 0.0, ALU.mult, ALU.add)\
                  .then_inc(s["split"], 1)
                gp.wait_ge(s["split"], 2 * e + 1)
                gp.tensor_tensor(out=WL[:, slot, 0:width], in0=WS[:, 0:width], in1=f(WH[:, slot, 0:width]),
                                 op=ALU.subtract).then_inc(s["split"], 1)

            def split_hidden(k, src):
                for t in range(NBLK):
                    if k in (3, 4):
                        gp.wait_ge(nrm_done, 4 * k + t + 1)
                    else:
                        gp.wait_ge(hn_done, 8 * centred(k) + 2 * t + 2)
                    gp.tensor_scalar(blk(HH, t), blk(src, t), 1.0, 0.0, ALU.mult, ALU.add).then_inc(hh_done, 1)

            def experts(n, ne, width):
                s = moe[n]

                def acc(m, t, e=None):
                    gp.wait_ge(s["ymul"], m + 1)
                    if e is not None:
                        gp.wait_ge(s["w_in"], 16 * (e + 1))
                    if not isinstance(m, int) or m > 0:
                        gp.wait_ge(s["acc"], m)
                    gp.tensor_tensor(out=blk(ACC, t), in0=blk(ACC, t), in1=YW[:, t % 2, :], op=ALU.add)\
                      .then_inc(s["acc"], 1)

                gp.wait_ge(s["acc_init"], 4)
                for m in range(8):
                    acc(m, m % 4, 2 + m // 4 if m % 4 == 3 else None)
                    if m % 4 == 3:
                        split_weights(n, 2 + m // 4, m // 4, width)
                with gp.Fori(1, 3) as it:
                    for u in range(8):
                        acc(8 * it + u, u % 4, 2 * it + 2 + u // 4 if u % 4 == 3 else None)
                        if u % 4 == 3:
                            split_weights(n, 2 * it + 2 + u // 4, u // 4, width)
                for m in range(24, 4 * ne):
                    acc(m, m % 4, 8 if m == 27 and ne == 9 else None)
                    if m == 27 and ne == 9:
                        split_weights(n, 8, 0, width)

            def lower(n, n0):
                for h in range(2):
                    if h == 0:
                        gp.wait_ge(exp_done, 3 * n + 2)
                    else:
                        gp.wait_ge(hi_done, n + 1)
                    if n0 >= 2:
                        gp.wait_ge(pv_done, n - 1)
                    gp.tensor_tensor(out=lower_of(n0, h), in0=PR[:, n0 % 2, 2 * h:2 * h + 2, :],
                                     in1=f(PH[:, n0 % 2, 2 * h:2 * h + 2, :]), op=ALU.subtract)\
                      .then_inc(lower_done, 1)

            for n in range(4):
                lower(n, n)
            with gp.Fori(0, 3) as it:
                for u in range(8):
                    lower(8 * it + 4 + u, 4 + u)
            for n in range(28, UNITS):
                lower(n, n)
            gp.wait_ge(pv_done, UNITS)
            for e in range(2):
                gp.wait_ge(moe[0]["w_in"], 16 * (e + 1))
                split_weights(0, e, e, 1024)
            split_hidden(1, HN)
            experts(0, E0, 1024)
            gp.wait_ge(moe[0]["y"], 4 * E0)
            for e in range(2):
                gp.wait_ge(moe[1]["w_in"], 16 * (e + 1))
                split_weights(1, e, e, 768)
            split_hidden(3, XC)
            split_hidden(4, XC)
            for t in range(NBLK):
                for c in range(3):
                    i = 3 * t + c
                    gp.wait_ge(pf_done, i + 1)
                    if t >= 2:
                        gp.wait_ge(z_psum, t - 1)
                    gp.tensor_scalar(GH[:, t % 2, c, :], PF[:, c, :], 1.0, 0.0, ALU.mult, ALU.add)\
                      .then_inc(ph_done, 1)
            split_hidden(5, HN)
            gp.wait_ge(x_upd, 12)
            gp.memset(ACC, 0.0).then_inc(moe[1]["acc_init"], 4)
            experts(1, E1, 768)

        @block.scalar
        def _(act):
            def norm_stats(k, src):
                eps = CON[:, 1:2] if k in (3, 4) else CON[:, 0:1]

                def square(t):
                    if k in (0, 1, 2, 5):
                        act.wait_ge(cen_done, 4 * centred(k) + t + 1)
                    elif k == 3:
                        act.wait_ge(hn_done, 16 + 2 * t + 2)
                    else:
                        act.wait_ge(hs2_done, t + 1)
                    if k > 0:
                        act.wait_ge(nrm_done, 4 * (k - 1) + t + 1)
                    act.activation(blk(STAT, t), blk(src, t), ACT.Square).then_inc(sq_done, 1)

                def inverse(t):
                    act.wait_ge(var_done, 4 * k + t + 1)
                    act.activation(blk(STAT, t), PS[:, 4 + t, :], ACT.Ln, bias=eps).then_inc(lnv_done, 1)
                    act.wait_ge(lnv_done, 4 * k + t + 1)
                    act.activation(blk(STAT, t), blk(STAT, t), ACT.Exp, scale=-0.5).then_inc(rstd_done, 1)

                act.preload_act_table_set("natural_log_exp_and_others")
                for t in range(NBLK):
                    square(t)
                    if t > 0:
                        inverse(t - 1)
                inverse(NBLK - 1)

            def router_exp(n):
                s = moe[n]
                act.wait_ge(s["lg"], 3)
                act.activation(RT["e"][:, :, :], RT["lg"][:, :, :], ACT.Exp).then_inc(s["exps"], 1)

            act.wait_ge(in_vec, 16)
            act.activation(SC[:, :], V[:, VAT["c"]:VAT["c"] + 16], ACT.Silu).then_inc(silu_done, 1)
            act.activation(SP[:, 0:1], vec("alpha"), ACT.Abs).then_inc(sp_done, 1)
            act.wait_ge(sp_done, 1)
            act.activation(SP[:, 1:2], SP[:, 0:1], ACT.Exp, scale=-1.0).then_inc(sp_done, 1)
            act.wait_ge(sp_done, 2)
            act.wait_ge(const_done, 4)
            act.activation(SP[:, 2:3], SP[:, 1:2], ACT.Ln, bias=CON[:, 2:3]).then_inc(sp_done, 1)
            norm_stats(0, XC)
            for t in range(NBLK):
                act.wait_ge(kd_done, t + 1)
                act.activation(LAT[:, t * BLK:(t + 1) * BLK], PS[0:64, t, :], ACT.Gelu, bias=vec("bkd")[0:64, :])\
                   .then_inc(lat_done, 1)

            def evac_proj(n, g):
                act.wait_ge(proj_done, n + 1)
                if not (isinstance(n, int) and n == 0):
                    act.wait_ge(qx_ready, 2 * n)
                act.activation(QT[:, :], PS[:, 6, 0:256], ACT.Identity, bias=vec("bq", g)).then_inc(qk_evac, 1)
                act.activation(KT[:, :], PS[:, 6, 256:512], ACT.Identity, bias=vec("bk", g)).then_inc(qk_evac, 1)
                act.wait_ge(qk_evac, 4 * n + 2)
                act.activation(QR, QT[:, :], ACT.Copy, scale=vec("q_sign")).then_inc(qk_evac, 1)
                act.activation(KR, KT[:, :], ACT.Copy, scale=vec("k_sign")).then_inc(qk_evac, 1)

            def exps(n, n0):
                for h in range(2):
                    act.wait_ge(st_done, 2 * n + h + 1)
                    if n0 >= 2:
                        act.wait_ge(pv_done, n - 1)
                    for out in (PR, PH)[:2 - h]:
                        act.activation(out[:, n0 % 2, 2 * h:2 * h + 2, :], PS[:, 2 + 2 * h:4 + 2 * h, 0:384],
                                       ACT.Exp, scale=SCALE).then_inc(exp_done, 1)

            def evac_out(n, n0):
                act.wait_ge(pv_done, n + 1)
                if n0 >= 2:
                    act.wait_ge(on_done, n - 1)
                act.activation(OT[:, n0 % 2, :], PS[:, 7, 0:256], ACT.Copy).then_inc(ot_done, 1)

            def recip(n, n0):
                act.wait_ge(su_done, n + 1)
                act.activation(SU[:, n0 % 2, :], SU[:, n0 % 2, :], ACT.Ln).then_inc(ls_done, 1)
                act.wait_ge(ls_done, n + 1)
                act.activation(SU[:, n0 % 2, :], SU[:, n0 % 2, :], ACT.Exp, scale=-1.0).then_inc(rsx_done, 1)

            def step(n0, it=0):
                n = n0 + 8 * it
                if n0 >= 2:
                    evac_out(n - 2, n0 - 2)
                exps(n, n0)
                if n0 + 3 < UNITS:
                    evac_proj(n + 3, (n0 + 3) % 4)
                if n0 >= 2:
                    recip(n - 2, n0 - 2)

            act.preload_act_table_set("natural_log_exp_and_others")
            evac_proj(0, 0)
            evac_proj(1, 1)
            evac_proj(2, 2)
            for n in range(4):
                step(n)
            with act.Fori(0, 3) as it:
                for u in range(8):
                    step(4 + u, it)
            for n in range(28, UNITS):
                step(n)
            for n in (30, 31):
                evac_out(n, n)
                recip(n, n)

            norm_stats(1, XC)
            router_exp(0)
            s = moe[0]

            def gelus(m, m0, e):
                for c in range(4):
                    act.wait_ge(s["h"], 4 * m + c + 1)
                    if m0 >= 1:
                        act.wait_ge(s["lo"], 4 * m - 4 + c + 1)
                    if m0 >= 2:
                        act.wait_ge(s["y"], m - 1)
                    if m0 % 4 == 0 and c == 0:
                        act.wait_ge(bias_done, e + 1)
                    bias = BI[:, m0 // 4 % 2, c:c + 1]
                    act.activation(G[:, c, :], PS[:, c, :], ACT.Gelu_apprx_tanh, bias=bias).then_inc(s["act"], 1)
                    act.activation(GH[:, m0 % 2, c, :], PS[:, c, :], ACT.Gelu_apprx_tanh, bias=bias)\
                       .then_inc(s["act"], 1)
                    if m0 % 4 == 3 and c == 0 and m0 < 35:
                        act.activation(BI[:, (m0 // 4 + 1) % 2, :], V[:, bass.ds(VAT["b1"] + 4 * e + 4, 4)],
                                       ACT.Copy).then_inc(bias_done, 1)

            act.activation(BI[:, 0, :], V[:, VAT["b1"]:VAT["b1"] + 4], ACT.Copy).then_inc(bias_done, 1)
            for m in range(8):
                gelus(m, m, m // 4)
            with act.Fori(1, 4) as it:
                for u in range(8):
                    gelus(8 * it + u, 8 + u, 2 * it + u // 4)
            for m in range(32, 36):
                gelus(m, m, 8)

            norm_stats(2, XC)
            norm_stats(3, HN)
            for i in range(16):
                p, t = i // 4, i % 4
                act.wait_ge(p1_psum, i + 1)
                func = (ACT.Sigmoid, ACT.Sigmoid, ACT.Gelu, ACT.Identity)[p]
                act.activation(blk((R_, I_, GATE, HS)[p], t), PS[:, i % 8, :], func, bias=vec("pb", p))\
                   .then_inc(p1_done, 1)
            act.wait_ge(sp_done, 5)
            for t in range(NBLK):
                act.wait_ge(p1_done, t + 1)
                act.activation(blk(A_, t), blk(R_, t), ACT.Exp, scale=SP[:, 3:4]).then_inc(a_done, 1)
            for t in range(NBLK):
                act.wait_ge(sa_done, 2 * t + 2)
                act.activation(blk(SA, t), blk(SA, t), ACT.Sqrt, bias=CON[:, 2:3]).then_inc(sqrt_done, 1)
            norm_stats(4, H2)
            for t in range(NBLK):
                for c in range(3):
                    i = 3 * t + c
                    act.wait_ge(mlp_psum, i + 1)
                    if t >= 1:
                        act.wait_ge(pf_done, i - 2)
                    act.activation(GG[:, c, :], PS[:, c, :], ACT.Gelu, bias=vec("gb", c)).then_inc(gg_done, 1)

            norm_stats(5, XC)
            router_exp(1)
            s1 = moe[1]

            def silus(m, m0):
                for c in range(2):
                    act.wait_ge(s1["h"], 2 * m + c + 1)
                    if m0 >= 1:
                        act.wait_ge(s1["prod"], 2 * m - 2 + c + 1)
                    act.activation(SG[:, c, :], PS[:, c, :], ACT.Silu).then_inc(s1["act"], 1)
                for c in range(2):
                    act.wait_ge(s1["prod"], 2 * m + c + 1)
                    if m0 >= 2:
                        act.wait_ge(s1["y"], m - 1)
                    act.activation(GH[:, m0 % 2, c, :], G[:, c, :], ACT.Copy).then_inc(s1["gh"], 1)

            for m in range(8):
                silus(m, m)
            with act.Fori(1, 4) as it:
                for u in range(8):
                    silus(8 * it + u, 8 + u)

        @block.vector
        def _(dve):
            def centre(k):
                for t in range(NBLK):
                    dve.wait_ge(mean_done, 4 * centred(k) + t + 1)
                    dve.tensor_tensor(out=blk(XC, t), in0=blk(X, t), in1=PS[:, t, :], op=ALU.subtract)\
                       .then_inc(cen_done, 1)

            def normalise(k):
                layer, which = k // 2 if k < 5 else 1, {0: 0, 1: 1, 2: 0, 5: 1}[k]
                for t in range(NBLK):
                    dve.wait_ge(rstd_done, 4 * k + t + 1)
                    dve.tensor_tensor(out=blk(HN, t), in0=blk(XC, t), in1=blk(STAT, t), op=ALU.mult)\
                       .then_inc(nrm_done, 1)
                    dve.wait_ge(nrm_done, 4 * k + t + 1)
                    for b in (2 * t, 2 * t + 1):
                        dve.tensor_scalar(blk(HN, b, SEQ), blk(HN, b, SEQ), MC[:, layer, which, b:b + 1],
                                          MOD[:, layer, 3 * which, b:b + 1], ALU.mult, ALU.add)\
                           .then_inc(hn_done, 1)

            def rms(k, src, weight):
                for t in range(NBLK):
                    dve.wait_ge(rstd_done, 4 * k + t + 1)
                    dve.scalar_tensor_tensor(out=blk(XC, t), in0=blk(src, t), scalar=vec(weight),
                                             in1=blk(STAT, t), op0=ALU.mult, op1=ALU.mult)\
                       .then_inc(nrm_done, 1)

            def rest(k, src):
                for t in range(NBLK):
                    dve.wait_ge(hh_done, 4 * split_at(k) + t + 1)
                    dve.tensor_tensor(out=blk(HL, t), in0=blk(src, t), in1=f(blk(HH, t)), op=ALU.subtract)\
                       .then_inc(hl_done, 1)

            def residual_acc(n, s, ne):
                for t in range(NBLK):
                    dve.wait_ge(s["acc"], 4 * ne - 3 + t)
                    for b in (2 * t, 2 * t + 1):
                        ins = dve.scalar_tensor_tensor(out=blk(X, b, SEQ), in0=blk(ACC, b, SEQ),
                                                       scalar=MG[:, n, 1, b:b + 1], in1=blk(X, b, SEQ),
                                                       op0=ALU.mult, op1=ALU.add)
                    ins.then_inc(x_upd, 1)

            def route(n, ne):
                s = moe[n]
                count = [0]
                lg, e, k1, k2, e2, w = (RT[k][:, :, :] for k in ("lg", "e", "k1", "k2", "e2", "w"))
                m, m1, km1, m2, km2, den = (RM[k][:, :] for k in ("m", "m1", "km1", "m2", "km2", "den"))
                prio = V[:, VAT["prio"]:VAT["prio"] + 8].unsqueeze(1).to_broadcast([128, 16, 8])

                def each(x):
                    return x.unsqueeze(2).to_broadcast([128, 16, 8])

                def link(ins, name="rstep"):
                    count[0] += name == "rstep"
                    ins.then_inc(s[name], 1)
                    if name == "rstep":
                        dve.wait_ge(s[name], count[0])

                dve.wait_ge(s["logits"], 1)
                lp = PS[:, 0, 0:128].rearrange("p (i e) -> p i e", e=8)
                if n == 0:
                    rb = ROWS[:, 128:136].unsqueeze(1).to_broadcast([128, 16, 8])
                    dve.wait_ge(in_rows, 32)
                    dve.tensor_tensor(out=lg, in0=lp, in1=rb, op=ALU.add).then_inc(s["lg"], 1)
                else:
                    dve.tensor_copy(lg, lp).then_inc(s["lg"], 1)
                dve.wait_ge(s["lg"], 1)
                dve.tensor_reduce(m, lg, axis=AX.X, op=ALU.max).then_inc(s["lg"], 1)
                dve.wait_ge(s["lg"], 2)
                dve.tensor_tensor(out=lg, in0=lg, in1=each(m), op=ALU.subtract).then_inc(s["lg"], 1)
                dve.wait_ge(s["exps"], 1)
                link(dve.tensor_reduce(m1, e, axis=AX.X, op=ALU.max))
                link(dve.tensor_tensor(out=k1, in0=e, in1=each(m1), op=ALU.is_equal))
                link(dve.tensor_tensor(out=k1, in0=k1, in1=prio, op=ALU.mult))
                link(dve.tensor_reduce(km1, k1, axis=AX.X, op=ALU.max))
                link(dve.tensor_tensor(out=k1, in0=k1, in1=each(km1), op=ALU.is_equal))
                link(dve.scalar_tensor_tensor(out=e2, in0=k1, scalar=-2.0, in1=e, op0=ALU.mult, op1=ALU.add))
                link(dve.tensor_reduce(m2, e2, axis=AX.X, op=ALU.max))
                link(dve.tensor_tensor(out=k2, in0=e2, in1=each(m2), op=ALU.is_equal))
                link(dve.tensor_tensor(out=k2, in0=k2, in1=prio, op=ALU.mult))
                link(dve.tensor_reduce(km2, k2, axis=AX.X, op=ALU.max))
                link(dve.tensor_tensor(out=k2, in0=k2, in1=each(km2), op=ALU.is_equal))
                link(dve.tensor_tensor(out=k1, in0=k1, in1=k2, op=ALU.add))
                link(dve.tensor_tensor(out=w, in0=k1, in1=e, op=ALU.mult))
                link(dve.tensor_tensor(out=den, in0=m1, in1=m2, op=ALU.add))
                link(dve.reciprocal(den, den))
                dve.tensor_tensor(out=COMB[:, :, 0:8], in0=w, in1=each(den), op=ALU.mult).then_inc(s["comb"], 1)
                if ne == 9:
                    dve.memset(COMB[:, :, 8:9], 1.0).then_inc(s["comb"], 1)
                for t in range(NBLK):
                    dve.wait_ge(s["combT"], t + 1)
                    dve.tensor_copy(CT[0:ne, t * BLK:(t + 1) * BLK], PS[0:ne, t, :]).then_inc(s["ct"], 1)

            def moe_scale(s, m, m0, pair, slot):
                dve.wait_ge(s["y"], m + 1)
                dve.wait_ge(s[f"wb_in{slot}"], 16 * (pair + 1))
                if m0 >= 2:
                    dve.wait_ge(s["acc"], m - 1)
                t = m0 % 4
                dve.tensor_tensor(out=YW[:, m0 % 2, :], in0=PS[:, 4 + m0 % 2, :],
                                  in1=WB[:, slot, t * BLK:(t + 1) * BLK], op=ALU.mult).then_inc(s["ymul"], 1)

            dve.wait_ge(mod_psum, 1)
            mp = PS[:, 7, 0:96].rearrange("p (l i b) -> p l i b", l=2, i=6)
            dve.tensor_copy(MOD[:, :, :, :], mp).then_inc(mod_done, 1)
            dve.tensor_scalar(MC[:, :, :, :], mp[:, :, 1::3, :], 1.0, None, ALU.add).then_inc(mod_done, 1)
            dve.wait_ge(mod_done, 2)
            gates = MOD[:, :, 2::3, :]
            dve.tensor_scalar(GS[:, :, :, :], gates, 0.0, 2.0, ALU.is_ge, ALU.mult).then_inc(gate_done, 1)
            for layer in range(2):
                dve.scalar_tensor_tensor(out=GA[:, layer, :, :], in0=gates[:, layer, :, :], scalar=-1.0,
                                         in1=gates[:, layer, :, :], op0=ALU.mult, op1=ALU.max)\
                   .then_inc(gate_done, 1)
            dve.wait_ge(gate_done, 3)
            dve.tensor_scalar(GA[:, :, :, :], GA[:, :, :, :], 0.25, None, ALU.max).then_inc(gate_done, 1)
            dve.wait_ge(gate_done, 4)
            dve.scalar_tensor_tensor(out=MG[:, :, :, :].rearrange("p l w b -> p (l w b)"),
                                     in0=GS[:, :, :, :].rearrange("p l w b -> p (l w b)"), scalar=-1.0,
                                     in1=GA[:, :, :, :].rearrange("p l w b -> p (l w b)"),
                                     op0=ALU.add, op1=ALU.mult).then_inc(gate_done, 1)
            dve.wait_ge(sp_done, 3)
            dve.scalar_tensor_tensor(out=SP[:, 3:4], in0=vec("alpha"), scalar=0.0, in1=SP[:, 2:3],
                                     op0=ALU.max, op1=ALU.add).then_inc(sp_done, 1)
            dve.wait_ge(sp_done, 4)
            dve.tensor_scalar(SP[:, 3:4], SP[:, 3:4], -8.0, None, ALU.mult).then_inc(sp_done, 1)

            centre(0)
            normalise(0)
            dve.wait_ge(in_rows, 32)
            for j in range(4):
                dve.wait_ge(v_psum, j + 1)
                dve.tensor_tensor(out=VALL[:, 4 * j:4 * j + 4, :],
                                  in0=PS[:, 4 + j, :].rearrange("p (i c) -> p i c", i=4),
                                  in1=ROWS[:, 0:128].unsqueeze(1).to_broadcast([128, 4, 128]), op=ALU.add)\
                   .then_inc(vall_done, 1)

            def join(n, g):
                dve.wait_ge(qk_evac, 4 * n + 4)
                if not isinstance(n, int) or n >= 4:
                    dve.wait_ge(st_done, 2 * n - 6)
                dve.scalar_tensor_tensor(out=QX[:, g, :], in0=QT[:, :], scalar=vec("q_keep"), in1=f(QR),
                                         op0=ALU.mult, op1=ALU.add).then_inc(qx_ready, 1)
                dve.scalar_tensor_tensor(out=KX[:, g, :], in0=KT[:, :], scalar=vec("k_keep"), in1=f(KR),
                                         op0=ALU.mult, op1=ALU.add).then_inc(qx_ready, 1)

            nmv = NM[:, :].rearrange("p (q j) -> p q j", q=2)

            def maxima(n, n0, h):
                dve.wait_ge(s_done, 2 * n + h + 1)
                if h == 0 and n0 >= 1:
                    dve.wait_ge(mp_ready, 2 * n)
                for q, keys in enumerate((slice(0, 128), slice(128, 384))):
                    dve.tensor_reduce(nmv[:, q, 2 * h:2 * h + 2], PS[:, 0:2, keys], axis=AX.X, op=ALU.max,
                                      negate=True).then_inc(max_done, 1)

            def spread_max(n, n0):
                dve.wait_ge(max_done, 4 * n + 4)
                dve.tensor_copy(NMH, NM[:, :]).then_inc(nmh_done, 1)
                dve.wait_ge(nmh_done, n + 1)
                if n0 >= 1:
                    dve.wait_ge(mt_done, n)
                dve.tensor_copy(MP[:, :, 24::32], f(NMH).rearrange("p (q j) -> p q j", q=2)).then_inc(mp_ready, 1)
                dve.tensor_tensor(out=MP[:, :, 25::32], in0=nmv, in1=f(NMH).rearrange("p (q j) -> p q j", q=2),
                                  op=ALU.subtract).then_inc(mp_ready, 1)

            def with_max(n, n0):
                dve.wait_ge(mt_done, n + 1)
                if n0 >= 2:
                    dve.wait_ge(st_done, 2 * n - 2)
                dve.tensor_tensor(out=QM[:, n0 % 2, :], in0=f(QX[:, n0 % 4, :]), in1=PS[:, 7, 256:512], op=ALU.add)\
                   .then_inc(qm_ready, 1)

            def spread_sum(n, n0):
                if n0 == 0:
                    dve.wait_ge(ot_done, n + 1)
                dve.stream_shuffle(SU[:, n0 % 2, :], OT[:, n0 % 2, :], [16] * 32).then_inc(su_done, 1)

            def divide(n, n0, it):
                dve.wait_ge(rsx_done, n + 1)
                if n0 + 1 < UNITS:
                    dve.wait_ge(ot_done, n + 2)
                if n0 >= 1:
                    dve.wait_ge(on_done, n)
                dve.tensor_tensor(out=ON[:, n0 % 4, bass.ds((2 * it + n0 // 4) * SEQ, SEQ)],
                                  in0=OT[:, n0 % 2, :], in1=SU[:, n0 % 2, :], op=ALU.mult).then_inc(on_done, 1)

            def place_values(b, b0):
                if b0 >= 1:
                    dve.wait_ge(pv_done, 4 * b)
                for kt in range(2):
                    own = VALL[:, bass.ds(2 * b + kt, 1), :].rearrange("p a (h c) -> p (a h) c", c=8)
                    dve.tensor_copy(values_of(kt, 0, 8), own).then_inc(vx_ready, 1)
                dve.wait_ge(vx_ready, 4 * b + 2)
                for kt in range(2):
                    own = VALL[:, bass.ds(2 * b + kt, 1), :].rearrange("p a (h c) -> p (a h) c", c=8)
                    dve.tensor_tensor(out=values_of(kt, 8, 16), in0=own, in1=f(values_of(kt, 0, 8)),
                                      op=ALU.subtract).then_inc(vx_ready, 1)

            def upper(n, n0):
                dve.wait_ge(exp_done, 3 * n + 3)
                if n0 >= 2:
                    dve.wait_ge(pv_done, n - 1)
                dve.tensor_copy(PH[:, n0 % 2, 2:4, :], PR[:, n0 % 2, 2:4, :]).then_inc(hi_done, 1)

            def step(n0, it=0):
                n = n0 + 8 * it
                if n0 % 4 == 1 and n0 > 1:
                    place_values(2 * it + n0 // 4, n0 // 4)
                if n0 + 1 < UNITS:
                    maxima(n + 1, n0 + 1, 1)
                    spread_max(n + 1, n0 + 1)
                if n0 >= 3:
                    divide(n - 3, n0 - 3, it)
                if n0 >= 2:
                    spread_sum(n - 2, n0 - 2)
                if n0 + 1 < UNITS:
                    with_max(n + 1, n0 + 1)
                if n0 + 2 < UNITS:
                    maxima(n + 2, n0 + 2, 0)
                upper(n, n0)
                if n0 + 3 < UNITS:
                    join(n + 3, (n0 + 3) % 4)

            dve.wait_ge(ones_done, 4)
            dve.wait_ge(vall_done, 4)
            place_values(0, 0)
            dve.wait_ge(ident_done, 9)
            join(0, 0)
            maxima(0, 0, 0)
            maxima(0, 0, 1)
            spread_max(0, 0)
            join(1, 1)
            with_max(0, 0)
            maxima(1, 1, 0)
            join(2, 2)
            for n in range(4):
                step(n)
            with dve.Fori(0, 3) as it:
                for u in range(8):
                    step(4 + u, it)
            for n in range(28, UNITS):
                step(n)
            divide(29, 29, 0)
            spread_sum(30, 30)
            divide(30, 30, 0)
            spread_sum(31, 31)
            divide(31, 31, 0)
            for t in range(NBLK):
                dve.wait_ge(wo_done, t + 1)
                for b in (2 * t, 2 * t + 1):
                    dve.tensor_scalar(blk(XC, b, SEQ), PS[:, t, (b % 2) * SEQ:(b % 2 + 1) * SEQ], vec("bo"),
                                      MG[:, 0, 0, b:b + 1], ALU.add, ALU.mult).then_inc(y_scaled, 1)
                dve.wait_ge(y_scaled, 2 * t + 2)
                dve.tensor_tensor(out=blk(X, t), in0=blk(X, t), in1=blk(XC, t), op=ALU.add).then_inc(x_upd, 1)

            centre(1)
            normalise(1)
            rest(1, HN)
            route(0, E0)
            s = moe[0]
            for t in range(NBLK):
                dve.wait_ge(s["b2_psum"], t + 1)
                dve.tensor_copy(blk(ACC, t), PS[:, 4 + t, :]).then_inc(s["acc_init"], 1)

            def lower0(m, m0):
                for c in range(4):
                    dve.wait_ge(s["act"], 2 * (4 * m + c + 1))
                    if m0 >= 2:
                        dve.wait_ge(s["y"], m - 1)
                    dve.tensor_tensor(out=GL[:, m0 % 2, c, :], in0=G[:, c, :], in1=f(GH[:, m0 % 2, c, :]),
                                      op=ALU.subtract).then_inc(s["lo"], 1)

            lower0(0, 0)
            for m in range(8):
                lower0(m + 1, m + 1)
                moe_scale(s, m, m, m // 8, m // 4 % 2)
            with dve.Fori(1, 4) as it:
                for u in range(8):
                    lower0(8 * it + u + 1, 9 + u)
                    moe_scale(s, 8 * it + u, 8 + u, it, u // 4)
            for m in range(32, 36):
                if m < 35:
                    lower0(m + 1, m + 1)
                moe_scale(s, m, m, 4, 0)
            residual_acc(0, s, E0)

            centre(2)
            normalise(2)
            rms(3, HN, "norm")
            rest(3, XC)
            for t in range(NBLK):
                dve.wait_ge(a_done, t + 1)
                dve.tensor_tensor(out=blk(SA, t), in0=blk(A_, t), in1=blk(A_, t), op=ALU.mult).then_inc(sa_done, 1)
                dve.wait_ge(sa_done, 2 * t + 1)
                dve.tensor_scalar(blk(SA, t), blk(SA, t), -1.0, -1.0, ALU.mult, ALU.max).then_inc(sa_done, 1)
            for t in range(NBLK):
                dve.wait_ge(p1_done, 12 + t + 1)
                dve.tensor_tensor(out=blk(HS, t), in0=blk(HS, t), in1=blk(I_, t), op=ALU.mult).then_inc(hsi_done, 1)
            for t in range(NBLK):
                dve.wait_ge(hsi_done, t + 1)
                dve.wait_ge(sqrt_done, t + 1)
                dve.tensor_tensor(out=blk(HS, t), in0=blk(HS, t), in1=blk(SA, t), op=ALU.mult).then_inc(s_ready, 1)
            for t in range(NBLK):
                dve.wait_ge(s_ready, t + 1)
                for b in (2 * t, 2 * t + 1):
                    dve.tensor_tensor_scan(out=blk(I_, b, SEQ), data0=blk(A_, b, SEQ), data1=blk(HS, b, SEQ),
                                           initial=0.0, op0=ALU.mult, op1=ALU.add).then_inc(scan_done, 1)
                dve.wait_ge(scan_done, 2 * t + 2)
                dve.tensor_tensor(out=blk(H2, t), in0=blk(I_, t), in1=blk(GATE, t), op=ALU.mult).then_inc(hs2_mul, 1)
                dve.wait_ge(hs2_mul, t + 1)
                dve.tensor_tensor(out=blk(H2, t), in0=blk(H2, t), in1=blk(HN, t), op=ALU.add).then_inc(hs2_done, 1)
            rms(4, H2, "norm2")
            rest(4, XC)

            def mlp_mid(t):
                for c in range(3):
                    i = 3 * t + c
                    dve.wait_ge(gg_done, i + 1)
                    if t >= 1:
                        dve.wait_ge(pl_done, i - 2)
                    dve.scalar_tensor_tensor(out=PF[:, c, :], in0=PS[:, 3 + c, :], scalar=vec("fb", c),
                                             in1=GG[:, c, :], op0=ALU.add, op1=ALU.mult).then_inc(pf_done, 1)
                for c in range(3):
                    i = 3 * t + c
                    dve.wait_ge(ph_done, i + 1)
                    dve.tensor_tensor(out=GL[:, t % 2, c, :], in0=PF[:, c, :], in1=f(GH[:, t % 2, c, :]),
                                      op=ALU.subtract).then_inc(pl_done, 1)

            def mlp_out(t):
                dve.wait_ge(z_psum, t + 1)
                dve.scalar_tensor_tensor(out=blk(XC, t), in0=PS[:, 6 + t % 2, :], scalar=vec("outb"),
                                         in1=blk(H2, t), op0=ALU.add, op1=ALU.add).then_inc(z_done, 1)
                dve.wait_ge(z_done, t + 1)
                for b in (2 * t, 2 * t + 1):
                    ins = dve.scalar_tensor_tensor(out=blk(X, b, SEQ), in0=blk(XC, b, SEQ),
                                                   scalar=MG[:, 1, 0, b:b + 1], in1=blk(X, b, SEQ),
                                                   op0=ALU.mult, op1=ALU.add)
                ins.then_inc(x_upd, 1)

            mlp_mid(0)
            for t in range(NBLK):
                if t < 3:
                    mlp_mid(t + 1)
                mlp_out(t)

            centre(5)
            normalise(5)
            rest(5, HN)
            route(1, E1)
            s1 = moe[1]

            def middle1(m, m0):
                for c in range(2):
                    dve.wait_ge(s1["act"], 2 * m + c + 1)
                    if m0 >= 1:
                        dve.wait_ge(s1["lo"], 2 * m - 2 + c + 1)
                    dve.tensor_tensor(out=G[:, c, :], in0=PS[:, 2 + c, :], in1=SG[:, c, :], op=ALU.mult)\
                       .then_inc(s1["prod"], 1)
                for c in range(2):
                    dve.wait_ge(s1["gh"], 2 * m + c + 1)
                    if m0 >= 2:
                        dve.wait_ge(s1["y"], m - 1)
                    dve.tensor_tensor(out=GL[:, m0 % 2, c, :], in0=G[:, c, :], in1=f(GH[:, m0 % 2, c, :]),
                                      op=ALU.subtract).then_inc(s1["lo"], 1)

            middle1(0, 0)
            for m in range(8):
                middle1(m + 1, m + 1)
                moe_scale(s1, m, m, m // 8, m // 4 % 2)
            with dve.Fori(1, 3) as it:
                for u in range(8):
                    middle1(8 * it + u + 1, 9 + u)
                    moe_scale(s1, 8 * it + u, 8 + u, it, u // 4)
            for m in range(24, 32):
                if m < 31:
                    middle1(m + 1, m + 1)
                moe_scale(s1, m, m, m // 8, m // 4 % 2)
            residual_acc(1, s1, E1)

        @block.tensor
        def _(pe):
            def three(out, wh, wl, xh, xl, first, last):
                pe.matmul(out, wh, xh, start=first, stop=False)
                pe.matmul(out, wl, xh, start=False, stop=False)
                return pe.matmul(out, wh, xl, start=False, stop=last)

            def means(k):
                for t in range(NBLK):
                    if k == 0:
                        pe.wait_ge(in_x, 16 * NBLK)
                    else:
                        pe.wait_ge(x_upd, 4 * centred(k) + t - 3)
                    pe.matmul(PS[:, t, :], OND[:, :], blk(X, t), start=True, stop=True).then_inc(mean_done, 1)

            def variances(k):
                for t in range(NBLK):
                    pe.wait_ge(sq_done, 4 * k + t + 1)
                    pe.matmul(PS[:, 4 + t, :], OND[:, :], blk(STAT, t), start=True, stop=True)\
                      .then_inc(var_done, 1)

            def router(n, name, ne):
                s = moe[n]
                pe.wait_ge(cen_done, 4 * centred(1 if n == 0 else 5) + 4)
                for i in range(16):
                    if i % 4 == 0:
                        pe.wait_ge(hn_done, 8 * centred(1 if n == 0 else 5) + i // 2 + 2)
                    mm = pe.matmul(PS[:, 0, 8 * i:8 * i + 8], HN[:, 128 * i:128 * i + 128], mat(name, 0, 8),
                                   start=True, stop=True)
                mm.then_inc(s["logits"], 1)
                return s

            def routes_out(n, ne):
                s = moe[n]
                pe.wait_ge(s["comb"], 2 if ne == 9 else 1)
                for i in range(16):
                    mm = pe.transpose(PS[0:ne, i // 4, 128 * (i % 4):128 * (i % 4) + 128], COMB[:, i, 0:ne],
                                      IDF[:, :])
                    if i % 4 == 3:
                        mm.then_inc(s["combT"], 1)

            pe.wait_ge(in_mod, 16)
            pe.wait_ge(silu_done, 1)
            for layer in range(2):
                for i in range(6):
                    mm = pe.matmul(PS[:, 7, 48 * layer + 8 * i:48 * layer + 8 * i + 8],
                                   WMOD[:, 768 * layer + 128 * i:768 * layer + 128 * i + 128],
                                   SC[:, 8 * layer:8 * layer + 8], start=True, stop=True)
            mm.then_inc(mod_psum, 1)
            pe.wait_ge(const_done, 4)
            means(0)
            pe.wait_ge(mod_done, 2)
            variances(0)
            pe.wait_ge(in_mats, 16)
            for t in range(NBLK):
                pe.wait_ge(hn_done, 2 * t + 2)
                pe.matmul(PS[0:64, t, :], mat("wkd", 0, 64), blk(HN, t), start=True, stop=True)\
                  .then_inc(kd_done, 1)
            pe.wait_ge(in_k, 16)
            for i in range(16):
                if i % 4 == 0:
                    pe.wait_ge(lat_done, i // 4 + 1)
                mm = pe.matmul(PS[:, 4 + i // 4, 128 * (i % 4):128 * (i % 4) + 128],
                               LAT[:, 128 * i:128 * i + 128], KM[:, 512:640], start=True, stop=True)
                if i % 4 == 3:
                    mm.then_inc(v_psum, 1)

            def project(n, n0, it):
                g, cols = n0 % 4, bass.ds((2 * it + n0 // 4) * SEQ, SEQ)
                if n0 >= 1:
                    pe.wait_ge(qk_evac, 4 * n)
                pe.matmul(PS[:, 6, 0:256], mat("wq", g), HN[:, cols], start=True, stop=True)
                pe.matmul(PS[:, 6, 256:512], KM[:, 128 * g:128 * g + 128], LAT[:, cols], start=True, stop=True)\
                  .then_inc(proj_done, 1)

            def diagonal(bank):
                return PS[:, bank, :].rearrange("p (a b) -> p a b", b=256)[:, :, 0:128]

            def mask(m):
                return m[:, :].unsqueeze(1).to_broadcast([128, 2, 128])

            def scores(n, n0, h):
                g = n0 % 4
                if h == 0:
                    pe.wait_ge(qx_ready, 2 * n + 2)
                    if n0 >= 1:
                        pe.wait_ge(max_done, 4 * n)
                else:
                    pe.wait_ge(max_done, 4 * n + 2)
                for j in range(2):
                    r = slice(64 * h + 32 * j, 64 * h + 32 * j + 32)
                    pe.matmul(PS[:, j, 0:128], QX[r, g, 0:128], KX[r, g, 0:128], start=True, stop=False)
                    pe.matmul(PS[:, j, 128:384], QX[r, g, 128:256], KX[r, g, :], start=False, stop=False)
                for j in range(2):
                    mm = pe.matmul(diagonal(j), IDB[:, :], mask(MKQ), start=False, stop=True)
                mm.then_inc(s_done, 1)

            def scores_t(n, n0, h):
                g = n0 % 4
                if h == 0:
                    pe.wait_ge(qm_ready, n + 1)
                if n0 >= 1:
                    pe.wait_ge(exp_done, 3 * n - 1 + h)
                for j in range(2):
                    r = slice(64 * h + 32 * j, 64 * h + 32 * j + 32)
                    bank = 2 + 2 * h + j
                    pe.matmul(PS[:, bank, 0:256], KX[r, g, 0:128], QM[r, n0 % 2, :], start=True, stop=False)
                    pe.matmul(PS[:, bank, 256:384], KX[r, g, 128:256], QM[r, n0 % 2, 128:256],
                              start=False, stop=False)
                for j in range(2):
                    mm = pe.matmul(diagonal(2 + 2 * h + j), IDB[:, :], mask(MKK), start=False, stop=True)
                mm.then_inc(st_done, 1)

            def values(n, n0, it):
                pe.wait_ge(lower_done, 2 * n + 2)
                pe.wait_ge(vx_ready, 4 * (2 * it + n0 // 4) + 4)
                if n0 >= 1:
                    pe.wait_ge(ot_done, n)
                if n0 + 2 < UNITS:
                    pe.wait_ge(qm_ready, n + 3)
                for j in range(4):
                    at = 128 * (4 * (n0 % 4) + j) + 96 - 32 * j
                    for i, part in enumerate((PH[:, n0 % 2, j, :], lower_of(n0, j // 2)[:, j % 2, :])):
                        first, last = i == j == 0, i == 1 and j == 3
                        pe.matmul(PS[:, 7, 0:256], VX[0][:, at:at + 128], part[:, 0:256],
                                  start=first, stop=False)
                        mm = pe.matmul(PS[:, 7, 128:256], VX[1][:, at:at + 128], part[:, 256:384],
                                       start=False, stop=last)
                mm.then_inc(pv_done, 1)

            def maxima_t(n, n0):
                pe.wait_ge(mp_ready, 2 * n + 2)
                if n0 >= 3:
                    pe.wait_ge(ot_done, n - 2)
                for q in range(2):
                    mm = pe.transpose(PS[:, 7, 256 + 128 * q:384 + 128 * q], MP[:, q, :], IDF[:, :])
                mm.then_inc(mt_done, 1)

            def step(n0, it=0):
                n = n0 + 8 * it
                if n0 + 1 < UNITS:
                    scores(n + 1, n0 + 1, 1)
                scores_t(n, n0, 0)
                scores_t(n, n0, 1)
                if n0 + 3 < UNITS:
                    project(n + 3, n0 + 3, it)
                if n0 + 1 < UNITS:
                    maxima_t(n + 1, n0 + 1)
                if n0 + 2 < UNITS:
                    scores(n + 2, n0 + 2, 0)
                if n0 >= 1:
                    values(n - 1, n0 - 1, it)

            pe.wait_ge(vall_done, 4)
            pe.wait_ge(ident_done, 9)
            def keep_clock(count):
                for _ in range(count):
                    pe.matmul(PS[:, 7, :], VX[0][:, 0:128], VX[0][:, 0:512], start=True, stop=True)

            pe.wait_ge(vx_ready, 4)
            project(0, 0, 0)
            scores(0, 0, 0)
            project(1, 1, 0)
            scores(0, 0, 1)
            project(2, 2, 0)
            keep_clock(4)
            maxima_t(0, 0)
            scores(1, 1, 0)
            pe.wait_ge(qm_ready, 1)
            keep_clock(4)
            step(0)
            pe.wait_ge(qm_ready, 2)
            keep_clock(4)
            for n in range(1, 4):
                step(n)
            with pe.Fori(0, 3) as it:
                for u in range(8):
                    step(4 + u, it)
            for n in range(28, UNITS):
                step(n)
            values(31, 31, 0)
            for t in range(NBLK):
                pe.wait_ge(on_done, 32)
                for g in range(4):
                    mm = pe.matmul(PS[:, t, :], mat("wo", g), ON[:, g, t * BLK:(t + 1) * BLK],
                                   start=(g == 0), stop=(g == 3))
                mm.then_inc(wo_done, 1)

            means(1)
            variances(1)
            router(0, "router", E0)
            routes_out(0, E0)
            s = moe[0]
            for t in range(NBLK):
                pe.wait_ge(s["ct"], t + 1)
                pe.matmul(PS[:, 4 + t, :], B2[:, :], CT[0:E0, t * BLK:(t + 1) * BLK], start=True, stop=True)\
                  .then_inc(s["b2_psum"], 1)

            def hidden0(m, m0, c):
                slot, t = m0 // 4 % 2, m0 % 4
                w = slice(128 * c, 128 * c + 128)
                if m0 >= 1:
                    pe.wait_ge(s["act"], 2 * (4 * m - 3 + c))
                three(PS[:, c, :], WH[:, slot, w], WL[:, slot, w], blk(HH, t), blk(HL, t), True, True)\
                    .then_inc(s["h"], 1)

            def output0(m, m0, c):
                slot = m0 // 4 % 2
                w = slice(512 + 128 * c, 640 + 128 * c)
                pe.wait_ge(s["lo"], 4 * m + c + 1)
                if c == 0 and m0 >= 2:
                    pe.wait_ge(s["ymul"], m - 1)
                mm = three(PS[:, 4 + m0 % 2, :], WH[:, slot, w], WL[:, slot, w], GH[:, m0 % 2, c, :],
                           GL[:, m0 % 2, c, :], c == 0, c == 3)
                if c == 3:
                    mm.then_inc(s["y"], 1)

            def step0(m, m0, e_next, ahead=True):
                if ahead and m0 % 4 == 3:
                    pe.wait_ge(s["split"], 2 * e_next + 2)
                for c in range(4):
                    if ahead:
                        hidden0(m + 1, m0 + 1, c)
                    output0(m, m0, c)

            pe.wait_ge(hl_done, 4)
            pe.wait_ge(s["split"], 2)
            pe.wait_ge(s["acc_init"], 4)
            for c in range(4):
                hidden0(0, 0, c)
            for m in range(8):
                step0(m, m, m // 4 + 1)
            with pe.Fori(1, 4) as it:
                for u in range(8):
                    step0(8 * it + u, 8 + u, 2 * it + u // 4 + 1)
            for m in range(32, 36):
                step0(m, m, 8, ahead=m < 35)

            means(2)
            variances(2)
            variances(3)
            pe.wait_ge(l1_split, 2)
            for i in range(16):
                p, t = i // 4, i % 4
                w = slice(128 * p, 128 * p + 128)
                pe.wait_ge(hl_done, 4 + t + 1)
                if i >= 8:
                    pe.wait_ge(p1_done, i - 7)
                elif i >= 4:
                    pe.wait_ge(lnv_done, 16)
                three(PS[:, i % 8, :], LH[:, w], LL[:, w], blk(HH, t), blk(HL, t), True, True)\
                    .then_inc(p1_psum, 1)
            pe.wait_ge(p1_done, 16)
            variances(4)

            def mlp_hidden(t):
                for c in range(3):
                    i = 3 * t + c
                    pe.wait_ge(hl_done, 8 + t + 1)
                    if t >= 1:
                        pe.wait_ge(pf_done, i - 2)
                    for which in range(2):
                        w = slice(512 + 384 * which + 128 * c, 640 + 384 * which + 128 * c)
                        mm = three(PS[:, 3 * which + c, :], LH[:, w], LL[:, w], blk(HH, t), blk(HL, t), True, True)
                    mm.then_inc(mlp_psum, 1)

            def mlp_output(t):
                if t >= 2:
                    pe.wait_ge(z_done, t - 1)
                for c in range(3):
                    pe.wait_ge(pl_done, 3 * t + c + 1)
                    w = slice(1280 + 128 * c, 1408 + 128 * c)
                    mm = three(PS[:, 6 + t % 2, :], LH[:, w], LL[:, w], GH[:, t % 2, c, :], GL[:, t % 2, c, :],
                               c == 0, c == 2)
                mm.then_inc(z_psum, 1)

            pe.wait_ge(lnv_done, 20)
            mlp_hidden(0)
            for t in range(NBLK):
                if t < 3:
                    mlp_hidden(t + 1)
                mlp_output(t)

            means(5)
            variances(5)
            router(1, "wg", E1)
            routes_out(1, E1)
            s1 = moe[1]

            def hidden1(m, m0, c):
                slot, t = m0 // 4 % 2, m0 % 4
                if m0 >= 1:
                    pe.wait_ge(s1["act"], 2 * m - 1 + c)
                    pe.wait_ge(s1["prod"], 2 * m - 1 + c)
                for which in range(2):
                    w = slice(256 * which + 128 * c, 256 * which + 128 * c + 128)
                    mm = three(PS[:, 2 * which + c, :], WH[:, slot, w], WL[:, slot, w], blk(HH, t), blk(HL, t),
                               True, True)
                mm.then_inc(s1["h"], 1)

            def output1(m, m0, c):
                slot = m0 // 4 % 2
                w = slice(512 + 128 * c, 640 + 128 * c)
                pe.wait_ge(s1["lo"], 2 * m + c + 1)
                if c == 0 and m0 >= 2:
                    pe.wait_ge(s1["ymul"], m - 1)
                mm = three(PS[:, 4 + m0 % 2, :], WH[:, slot, w], WL[:, slot, w], GH[:, m0 % 2, c, :],
                           GL[:, m0 % 2, c, :], c == 0, c == 1)
                if c == 1:
                    mm.then_inc(s1["y"], 1)

            def step1(m, m0, e_next, ahead=True):
                if ahead and m0 % 4 == 3:
                    pe.wait_ge(s1["split"], 2 * e_next + 2)
                for c in range(2):
                    if ahead:
                        hidden1(m + 1, m0 + 1, c)
                    output1(m, m0, c)

            pe.wait_ge(hl_done, 16)
            pe.wait_ge(s1["split"], 2)
            pe.wait_ge(s1["ct"], 4)
            for c in range(2):
                hidden1(0, 0, c)
            for m in range(8):
                step1(m, m, m // 4 + 1)
            with pe.Fori(1, 3) as it:
                for u in range(8):
                    step1(8 * it + u, 8 + u, 2 * it + u // 4 + 1)
            for m in range(24, 32):
                step1(m, m, m // 4 + 1, ahead=m < 31)


def layouts(inputs):
    import numpy as np

    a = {k: np.asarray(v) for k, v in inputs.items()}
    f4 = np.float32

    def heads(v, parts):
        v = v.reshape(v.shape[:-1] + (4, 4, 1, 8))
        out = np.zeros(v.shape[:-2] + (4, 8), f4)
        out[..., :parts, :] = v
        return out.reshape(out.shape[:-4] + (4, 128))

    vecs = np.zeros((128, VN), f4)

    def put(name, v):
        v = v.reshape(v.shape[0], -1)
        vecs[:v.shape[0], VAT[name]:VAT[name] + v.shape[1]] = v

    bk = heads(a["L0_attn_bku"][:128], 3)
    for j in range(4):
        bk[:, 32 * j + 24:32 * j + 26] = 1.0
    row = np.arange(128) % 32 // 8
    b1 = np.concatenate([a["L0_ffn_spec_b1"], a["L0_ffn_shared_b1"][None]])
    put("bo", a["L0_attn_bo"])
    put("bq", heads(a["L0_attn_bq"], 3).T)
    put("bk", bk.T)
    put("q_sign", np.array([1, -1, 1, 1], f4)[row])
    put("q_keep", np.array([0, 1, 0, 0], f4)[row])
    put("k_sign", np.array([1, 1, -1, 1], f4)[row])
    put("k_keep", np.array([0, 0, 1, 0], f4)[row])
    put("b1", b1.reshape(E0, 4, 128).transpose(2, 0, 1))
    put("pb", np.stack([a[f"L1_attn_fc_{n}"] for n in ("r_b", "i_b", "gate_b", "b")], 1))
    put("gb", a["L1_attn_mlp_gate_b"].reshape(3, 128).T)
    put("fb", a["L1_attn_mlp_fc_b"].reshape(3, 128).T)
    put("outb", a["L1_attn_out_b"])
    put("alpha", a["L1_attn_alpha"].reshape(128))
    put("norm", a["L1_attn_norm_w"])
    put("norm2", a["L1_attn_norm2_w"])
    put("bkd", a["L0_attn_bkd"])
    put("c", np.concatenate([a["L0_c"], a["L1_c"]]).T)
    put("prio", np.tile(np.arange(8, 0, -1, dtype=f4), (128, 1)))

    wo = np.zeros((128, 4, 128), f4)
    for j in range(4):
        rows = a["L0_attn_Wo"].reshape(4, 4, 8, 128)[:, j].transpose(1, 0, 2)
        wo[32 * j:32 * j + 16] = np.concatenate([rows, rows])
    l1 = [a[f"L1_attn_fc_{n}"].T for n in ("r_w", "i_w", "gate_w", "w")]
    l1 += [a["L1_attn_mlp_gate_w"].T, a["L1_attn_mlp_fc_w"].T,
           a["L1_attn_out_w"].T.reshape(3, 128, 128).transpose(1, 0, 2).reshape(128, 384)]
    mats = np.concatenate([a["L0_attn_Wkd"], heads(a["L0_attn_Wq"], 3).reshape(128, 512), wo.reshape(128, 512),
                           a["L0_ffn_router_w"].T, a["L1_ffn_Wg"]] + l1, 1)
    wk = np.concatenate([heads(a["L0_attn_Wku"][:, :128], 3).reshape(32, 512), a["L0_attn_Wku"][:, 128:]], 1)
    rows = np.concatenate([a["L0_attn_bku"][128:], a["L0_ffn_router_b"]])
    up = np.concatenate([a["L0_ffn_spec_w1"], a["L0_ffn_shared_w1"][None]]).transpose(0, 2, 1)
    down = np.concatenate([a["L0_ffn_spec_w2"], a["L0_ffn_shared_w2"][None]]).transpose(0, 2, 1)
    down = down.reshape(E0, 4, 128, 128).transpose(0, 2, 1, 3).reshape(E0, 128, 512)
    down1 = a["L1_ffn_W2"].reshape(E1, 2, 128, 128).transpose(0, 2, 1, 3).reshape(E1, 128, 256)
    return dict(
        xT=a["L0_attn_x"].reshape(TOK, D).T,
        wmod=np.concatenate([a["L0_wmod"], a["L1_wmod"]], 1),
        vecs=vecs,
        mats=mats,
        kmats=np.concatenate([wk, wk]),
        rows=np.tile(rows, (128, 1)),
        b2=np.concatenate([a["L0_ffn_spec_b2"], a["L0_ffn_shared_b2"][None]]),
        w0=np.concatenate([up, down], 2),
        w1=np.concatenate([a["L1_ffn_W1"], a["L1_ffn_W3"], down1], 2),
    )


def kernel(**inputs):
    import numpy as np
    import concourse.bacc as bacc
    from concourse.bass_utils import run_bass_kernel_spmd

    nc = bacc.Bacc("TRN2", target_bir_lowering=False, num_devices=1)
    arrays, args = {}, []
    for name, value in layouts(inputs).items():
        value = np.ascontiguousarray(value)
        arrays[f"in_{name}"] = value
        args.append(nc.dram_tensor(f"in_{name}", value.shape, mybir.dt.from_np(value.dtype),
                                   kind="ExternalInput").ap())
    for n, ne in enumerate((E0, E1)):
        args.append(nc.dram_tensor(f"comb_{n}", (ne, TOK), mybir.dt.float32, kind="Internal").ap())
    args.append(nc.dram_tensor("out_xT", (D, TOK), mybir.dt.float32, kind="ExternalOutput").ap())
    build(nc, *args)
    r = run_bass_kernel_spmd(nc, [arrays], core_ids=[0])
    return np.ascontiguousarray(r.results[0]["out_xT"].T).reshape(BATCHES, SEQ, D)
```

```python
import concourse.bass as bass
from concourse import mybir
from contextlib import ExitStack

TOK, D, BATCHES, SEQ = 2048, 128, 8, 256
BLK, NBLK = 512, 4
HEADS, HD, GROUPS = 16, 8, 4
UNITS = BATCHES * GROUPS
E0, F0 = 9, 512
E1, F1 = 8, 256
SCALE = HD ** -0.5
MASKED = -1e30

VECS = dict(bo=1, bq=4, bk=4, q_sign=1, q_keep=1, k_sign=1, k_keep=1, b1=4 * E0, pb=4, gb=3, fb=3,
            outb=1, alpha=1, norm=1, norm2=1, bkd=1, c=16, prio=8)
MATS = dict(wkd=64, wq=512, wo=512, router=8, wg=8, l1=4 * 128 + 3 * 384)


def columns(widths):
    at, out = 0, {}
    for name, width in widths.items():
        out[name] = at
        at += width
    return out, at


VAT, VN = columns(VECS)
MAT_AT, MN = columns(MATS)


def build(nc, xT, wmod, vecs, mats, kmats, rows, b2, w0, w1, comb0, comb1, outT):
    f32, r32, bf16 = mybir.dt.float32, mybir.dt.float32r, mybir.dt.bfloat16
    ALU, ACT, AX = mybir.AluOpType, mybir.ActivationFunctionType, mybir.AxisListType
    ctx = ExitStack()
    with ctx:
        def sb(name, shape, dt=f32):
            return ctx.enter_context(nc.sbuf_tensor(name, shape, dt))

        def sem(name):
            return ctx.enter_context(nc.semaphore(name))

        def f(ap):
            return ap.bitcast(f32)

        def blk(tile, t, n=BLK):
            return tile[:, t * n:(t + 1) * n]

        X = sb("X", [128, TOK])
        HN = sb("HN", [128, TOK])
        HH = sb("HH", [128, TOK], r32)
        HL = sb("HL", [128, TOK], r32)
        XC = sb("XC", [128, TOK])
        STAT = sb("STAT", [128, TOK])
        AR = sb("AR", [128, 17408])
        RA = sb("RA", [128, 8192], r32)
        WS = sb("WS", [128, 1024])
        WH = sb("WH", [128, 2, 1024], r32)
        WL = sb("WL", [128, 2, 1024], r32)
        V = sb("V", [128, VN])
        M = sb("M", [128, MN])
        LH = sb("LH", [128, MATS["l1"]], r32)
        LL = sb("LL", [128, MATS["l1"]], r32)
        KM = sb("KM", [64, 640])
        ROWS = sb("ROWS", [128, 136])
        B2 = sb("B2", [E0, 128])
        MOD = sb("MOD", [128, 2, 6, 8])
        MC = sb("MC", [128, 2, 2, 8])
        GS = sb("GS", [128, 2, 2, 8])
        GA = sb("GA", [128, 2, 2, 8])
        MG = sb("MG", [128, 2, 2, 8])
        BI = sb("BI", [128, 2, 4])
        SC = sb("SC", [128, 16])
        CON = sb("CON", [128, 4])
        OND = sb("OND", [128, 128])
        IDF = sb("IDF", [128, 128])
        IDB = sb("IDB", [128, 128], bf16)
        MKQ = sb("MKQ", [128, 128], bf16)
        MKK = sb("MKK", [128, 128], bf16)
        SP = sb("SP", [128, 4])
        PS = ctx.enter_context(nc.psum_tensor("PS", [128, 8, 512], f32))

        def vec(name, i=0):
            return V[:, VAT[name] + i:VAT[name] + i + 1]

        def mat(name, i=0, n=128):
            return M[:, MAT_AT[name] + i * n:MAT_AT[name] + (i + 1) * n]

        WMOD = AR[:, 0:1536]
        ON = AR[:, 0:8192].rearrange("p (g n) -> p g n", g=4)
        LAT = AR[0:64, 8192:10240]
        VALL = AR[:, 10240:12288].rearrange("p (i c) -> p i c", i=16)
        PR = AR[:, 12288:15360].rearrange("p (r j n) -> p r j n", r=2, j=4)
        VX = (HH, HL)
        PL = (WH, WL)
        QX = RA[:, 0:1024].rearrange("p (g n) -> p g n", g=4)
        KX = RA[:, 1024:2048].rearrange("p (g n) -> p g n", g=4)
        QM = RA[:, 2048:2560].rearrange("p (r n) -> p r n", r=2)
        QR = RA[:, 2560:2816]
        KR = RA[:, 2816:3072]
        NMH = RA[:, 3072:3080]
        PH = RA[:, 3080:6152].rearrange("p (r j n) -> p r j n", r=2, j=4)
        QT = sb("QT", [128, 256])
        KT = sb("KT", [128, 256])
        NM = sb("NM", [128, 8])
        MP = sb("MP", [128, 2, 128])
        OT = sb("OT", [128, 2, 256])
        SU = sb("SU", [128, 2, 256])
        G = AR[:, 0:2048].rearrange("p (c n) -> p c n", c=4)
        SG = AR[:, 2048:3072].rearrange("p (c n) -> p c n", c=2)
        YW = AR[:, 3072:4096].rearrange("p (r n) -> p r n", r=2)
        ACC = AR[:, 4096:6144]
        WB = AR[:, 6144:10240].rearrange("p (r n) -> p r n", r=2)
        CT = AR[:, 10240:12288]
        GH = RA[:, 0:4096].rearrange("p (r c n) -> p r c n", r=2, c=4)
        GL = RA[:, 4096:8192].rearrange("p (r c n) -> p r c n", r=2, c=4)
        R_, I_, GATE, HS, A_, SA = (AR[:, 2048 * i:2048 * (i + 1)] for i in range(6))
        H2 = AR[:, 12288:14336]
        GG = AR[:, 14336:15872].rearrange("p (c n) -> p c n", c=3)
        PF = AR[:, 15872:17408].rearrange("p (c n) -> p c n", c=3)
        RT = {n: AR[:, 12288 + 128 * i:12416 + 128 * i].rearrange("p (i e) -> p i e", e=8)
              for i, n in enumerate(("lg", "e", "k1", "k2", "e2", "w"))}
        RM = {n: sb("RM_" + n, [128, 16]) for n in ("m", "m1", "km1", "m2", "km2", "den")}
        COMB = sb("COMB", [128, 16, E0])

        in_x = [sem(f"in_x{t}") for t in range(NBLK)]
        in_vec, in_mod, in_mats, in_k, in_rows = map(sem, ("in_vec", "in_mod", "in_mats", "in_k", "in_rows"))
        const_done, ident_done, silu_done, mod_psum, mod_done, gate_done, sp_done = map(
            sem, ("const_done", "ident_done", "silu_done", "mod_psum", "mod_done", "gate_done", "sp_done"))
        mean_done, cen_done, sq_done, var_done, lnv_done, rstd_done, nrm_done, hn_done, hh_done, hl_done = map(
            sem, ("mean_done", "cen_done", "sq_done", "var_done", "lnv_done", "rstd_done", "nrm_done",
                  "hn_done", "hh_done", "hl_done"))
        x_upd, y_scaled = sem("x_upd"), sem("y_scaled")
        out_done = sem("out_done")
        kd_done, lat_done, v_psum, vall_done, ones_done = map(
            sem, ("kd_done", "lat_done", "v_psum", "vall_done", "ones_done"))
        (proj_done, qk_evac, qx_ready, s_done, max_done, nmh_done, mp_ready, mt_done, qm_ready, st_done,
         exp_done, pv_done, ot_done, su_done, ls_done, rsx_done, on_done, vx_ready, wo_done) = map(
            sem, ("proj_done", "qk_evac", "qx_ready", "s_done", "max_done", "nmh_done", "mp_ready",
                  "mt_done", "qm_ready", "st_done", "exp_done", "pv_done", "ot_done", "su_done",
                  "ls_done", "rsx_done", "on_done", "vx_ready", "wo_done"))
        hi_done, lower_done = sem("hi_done"), sem("lower_done")
        l1_split = sem("l1_split")
        bias_done = sem("bias_done")
        p1_psum, p1_done, a_done, sa_done, hsi_done, sqrt_done, s_ready, scan_done, hs2_mul, hs2_done = map(
            sem, ("p1_psum", "p1_done", "a_done", "sa_done", "hsi_done", "sqrt_done", "s_ready", "scan_done",
                  "hs2_mul", "hs2_done"))
        ln_done = sem("ln_done")
        mlp_psum, gg_done, pf_done, ph_done, pl_done, z_psum, z_done = map(
            sem, ("mlp_psum", "gg_done", "pf_done", "ph_done", "pl_done", "z_psum", "z_done"))

        def moe_sems(n):
            names = ("logits", "lg", "exps", "rstep", "comb", "combT", "ct", "stored", "b2_psum", "acc_init",
                     "w_in", "split", "wb_in0", "wb_in1", "h", "act", "prod", "gh", "lo", "y", "ymul", "acc")
            return {k: sem(f"moe{n}_{k}") for k in names}

        moe = [moe_sems(0), moe_sems(1)]
        block = ctx.enter_context(nc.Block())

        def values_of(kt, a, b):
            return VX[kt][:, :].rearrange("p (h c) -> p h c", c=128)[:, :, 96 + a:96 + b]

        def lower_of(n0, h):
            return PL[n0 % 2][:, :, :].rearrange("p r n -> p (r n)")[:, 768 * h:768 * h + 768]\
                .rearrange("p (j n) -> p j n", j=2)

        def centred(k):
            return {0: 0, 1: 1, 2: 2, 5: 3}[k]

        turns = [(2, 0), (2, 1), (3, 0), (2, 2), (3, 1), (2, 3), (3, 2), (3, 3)]

        def norm_at(k, t):
            return 8 + turns.index((k, t)) if k in (2, 3) else 4 * k + t

        projected = [(p, t) for t in range(NBLK) for p in (0, 1, 3)] + [(2, t) for t in range(NBLK)]

        def evacuated(i):
            return sum(p != 3 for p, _ in projected[:i + 1])

        def variance_bank(k, t):
            return 6 + t % 2 if k == 4 else 4 + norm_at(k, t) % 2

        def split_at(k):
            return {1: 0, 3: 1, 4: 2, 5: 3}[k]

        @block.sync
        def _(sp):
            sp.dma_start(V[:, :], vecs).then_inc(in_vec, 16)
            for t in range(NBLK):
                sp.dma_start(blk(X, t), blk(xT, t)).then_inc(in_x[t], 16)
            sp.dma_start(WMOD, wmod).then_inc(in_mod, 16)
            sp.dma_start(KM[:, :], kmats).then_inc(in_k, 16)
            sp.dma_start(M[:, :], mats).then_inc(in_mats, 16)
            sp.dma_start(ROWS[:, :], rows).then_inc(in_rows, 16)
            sp.dma_start(B2[:, :], b2).then_inc(in_rows, 16)

            for n, (w, comb, ne, width) in enumerate(((w0, comb0, E0, 1024), (w1, comb1, E1, 768))):
                s = moe[n]

                for e in range(2):
                    if e == 1:
                        sp.wait_ge(s["split"], 2)
                    elif n == 1:
                        sp.wait_ge(moe[0]["split"], 2 * E0)
                    sp.dma_start(WS[:, 0:width], w[e, :, :]).then_inc(s["w_in"], 16)
                sp.wait_ge(s["ct"], 4)
                sp.dma_start(comb, CT[0:ne, :]).then_inc(s["stored"], 16)
                sp.wait_ge(s["stored"], 16)
                for e in range(2):
                    sp.dma_start(WB[:, e, :], comb[e:e + 1, :].to_broadcast([128, TOK])).then_inc(s[f"wb_in{e}"], 16)

                def later(e, slot):
                    sp.wait_ge(s["split"], 2 * e)
                    sp.dma_start(WS[:, 0:width], w[bass.ds(e, 1), :, :].rearrange("a p n -> p (a n)")).then_inc(s["w_in"], 16)
                    sp.wait_ge(s["ymul"], 4 * e - 4)
                    sp.dma_start(WB[:, slot, :], comb[bass.ds(e, 1), :].to_broadcast([128, TOK])).then_inc(s[f"wb_in{slot}"], 16)

                with sp.Fori(0, 3) as it:
                    for u in range(2):
                        later(2 * it + 2 + u, u)
                if ne == 9:
                    later(8, 0)

            for t in range(NBLK):
                sp.wait_ge(x_upd, 4 * 3 + t + 1)
                sp.dma_start(blk(outT, t), blk(X, t)).then_inc(out_done, 16)
            sp.wait_ge(out_done, 16 * NBLK)

        @block.gpsimd
        def _(gp):
            gp.memset(CON[:, 0:1], 1e-5).then_inc(const_done, 1)
            gp.memset(CON[:, 1:2], 1e-6).then_inc(const_done, 1)
            gp.memset(CON[:, 2:3], 1.0).then_inc(const_done, 1)
            gp.memset(OND[:, :], 1.0 / D).then_inc(const_done, 1)
            for m in (IDF, IDB, MKQ, MKK, MP):
                gp.memset(m[:], 0.0).then_inc(ident_done, 1)
            gp.wait_ge(ident_done, 5)
            for m in (IDF, IDB):
                gp.affine_select(out=m[:, :], in_=m[:, :], compare_op=ALU.not_equal, fill=1.0, base=0,
                                 pattern=[[-1, 128]], channel_multiplier=1).then_inc(ident_done, 1)
            gp.affine_select(out=MKQ[:, :], in_=MKQ[:, :], compare_op=ALU.is_ge, fill=MASKED, base=0,
                             pattern=[[-1, 128]], channel_multiplier=1).then_inc(ident_done, 1)
            gp.affine_select(out=MKK[:, :], in_=MKK[:, :], compare_op=ALU.is_ge, fill=MASKED, base=0,
                             pattern=[[1, 128]], channel_multiplier=-1).then_inc(ident_done, 1)
            for kt in range(2):
                gp.memset(f(VX[kt][:, :]), 0.0).then_inc(ones_done, 1)
            gp.wait_ge(ones_done, 2)
            for kt in range(2):
                gp.memset(f(values_of(kt, 16, 24)), 1.0).then_inc(ones_done, 1)
            gp.wait_ge(in_mats, 16)
            lm = M[:, MAT_AT["l1"]:MAT_AT["l1"] + MATS["l1"]]
            gp.tensor_scalar(LH[:, :], lm, 1.0, 0.0, ALU.mult, ALU.add).then_inc(l1_split, 1)
            gp.wait_ge(l1_split, 1)
            gp.tensor_tensor(out=LL[:, :], in0=lm, in1=f(LH[:, :]), op=ALU.subtract).then_inc(l1_split, 1)

            def split_weights(n, e, slot, width):
                s = moe[n]
                gp.tensor_scalar(WH[:, slot, 0:width], WS[:, 0:width], 1.0, 0.0, ALU.mult, ALU.add)\
                  .then_inc(s["split"], 1)
                gp.wait_ge(s["split"], 2 * e + 1)
                gp.tensor_tensor(out=WL[:, slot, 0:width], in0=WS[:, 0:width], in1=f(WH[:, slot, 0:width]),
                                 op=ALU.subtract).then_inc(s["split"], 1)

            def split_hidden(k, src, t):
                if k in (3, 4):
                    gp.wait_ge(nrm_done, norm_at(k, t) + 1)
                else:
                    gp.wait_ge(hn_done, 8 * centred(k) + 2 * t + 2)
                gp.tensor_scalar(blk(HH, t), blk(src, t), 1.0, 0.0, ALU.mult, ALU.add).then_inc(hh_done, 1)

            def experts(n, ne, width):
                s = moe[n]

                def acc(m, t, e=None):
                    gp.wait_ge(s["ymul"], m + 1)
                    if e is not None:
                        gp.wait_ge(s["w_in"], 16 * (e + 1))
                        gp.wait_ge(s["y"], m + 3)
                    if not isinstance(m, int) or m > 0:
                        gp.wait_ge(s["acc"], m)
                    gp.tensor_tensor(out=blk(ACC, t), in0=blk(ACC, t), in1=YW[:, t % 2, :], op=ALU.add)\
                      .then_inc(s["acc"], 1)

                gp.wait_ge(s["acc_init"], 4)
                for m in range(8):
                    acc(m, m % 4, 2 + m // 4 if m % 4 == 1 else None)
                    if m % 4 == 1:
                        split_weights(n, 2 + m // 4, m // 4, width)
                with gp.Fori(1, 3) as it:
                    for u in range(8):
                        acc(8 * it + u, u % 4, 2 * it + 2 + u // 4 if u % 4 == 1 else None)
                        if u % 4 == 1:
                            split_weights(n, 2 * it + 2 + u // 4, u // 4, width)
                for m in range(24, 4 * ne):
                    acc(m, m % 4, 8 if m == 25 and ne == 9 else None)
                    if m == 25 and ne == 9:
                        split_weights(n, 8, 0, width)

            def lower(n, n0):
                for h in range(2):
                    if h == 0:
                        gp.wait_ge(exp_done, 3 * n + 2)
                    else:
                        gp.wait_ge(hi_done, n + 1)
                    if n0 >= 2:
                        gp.wait_ge(pv_done, n - 1)
                    gp.tensor_tensor(out=lower_of(n0, h), in0=PR[:, n0 % 2, 2 * h:2 * h + 2, :],
                                     in1=f(PH[:, n0 % 2, 2 * h:2 * h + 2, :]), op=ALU.subtract)\
                      .then_inc(lower_done, 1)

            for n in range(4):
                lower(n, n)
            with gp.Fori(0, 3) as it:
                for u in range(8):
                    lower(8 * it + 4 + u, 4 + u)
            for n in range(28, UNITS):
                lower(n, n)
            gp.wait_ge(pv_done, UNITS)
            gp.wait_ge(moe[0]["w_in"], 16)
            split_weights(0, 0, 0, 1024)
            for t in range(NBLK):
                split_hidden(1, HN, t)
            for c in range(4):
                gp.wait_ge(moe[0]["act"], 2 * (c + 1))
                gp.tensor_tensor(out=GL[:, 0, c, :], in0=G[:, c, :], in1=f(GH[:, 0, c, :]), op=ALU.subtract)\
                  .then_inc(moe[0]["lo"], 1)
            gp.wait_ge(moe[0]["w_in"], 32)
            split_weights(0, 1, 1, 1024)
            experts(0, E0, 1024)
            gp.wait_ge(moe[0]["y"], 4 * E0)
            for e in range(2):
                gp.wait_ge(moe[1]["w_in"], 16 * (e + 1))
                split_weights(1, e, e, 768)
            for t in range(NBLK):
                split_hidden(3, XC, t)
            for t in range(NBLK):
                split_hidden(4, XC, t)
            for t in range(NBLK):
                for c in range(3):
                    i = 3 * t + c
                    gp.wait_ge(pf_done, i + 1)
                    if t >= 2:
                        gp.wait_ge(z_psum, t - 1)
                    gp.tensor_scalar(GH[:, t % 2, c, :], PF[:, c, :], 1.0, 0.0, ALU.mult, ALU.add)\
                      .then_inc(ph_done, 1)
            for t in range(NBLK):
                split_hidden(5, HN, t)
            gp.wait_ge(x_upd, 12)
            gp.memset(ACC, 0.0).then_inc(moe[1]["acc_init"], 4)
            experts(1, E1, 768)

        @block.scalar
        def _(act):
            def square(k, src, t):
                if k in (0, 1, 2, 5):
                    act.wait_ge(cen_done, 4 * centred(k) + t + 1)
                elif k == 3:
                    act.wait_ge(hn_done, 16 + 2 * t + 2)
                else:
                    act.wait_ge(hs2_done, t + 1)
                if k > 0:
                    act.wait_ge(nrm_done, norm_at(k - 1, t) + 1)
                act.activation(blk(STAT, t), blk(src, t), ACT.Square).then_inc(sq_done, 1)

            def inverse(k, t):
                eps = CON[:, 1:2] if k in (3, 4) else CON[:, 0:1]
                at = norm_at(k, t)
                act.wait_ge(var_done, at + 1)
                act.activation(blk(STAT, t), PS[:, variance_bank(k, t), :], ACT.Ln, bias=eps).then_inc(lnv_done, 1)
                act.wait_ge(lnv_done, at + 1)
                act.activation(blk(STAT, t), blk(STAT, t), ACT.Exp, scale=-0.5).then_inc(rstd_done, 1)

            def norm_stats(k, src):
                act.preload_act_table_set("natural_log_exp_and_others")
                for t in range(NBLK):
                    square(k, src, t)
                    if t > 0:
                        inverse(k, t - 1)
                inverse(k, NBLK - 1)

            def router_exp(n):
                s = moe[n]
                act.wait_ge(s["lg"], 3)
                act.activation(RT["e"][:, :, :], RT["lg"][:, :, :], ACT.Exp).then_inc(s["exps"], 1)

            act.wait_ge(in_vec, 16)
            act.activation(SC[:, :], V[:, VAT["c"]:VAT["c"] + 16], ACT.Silu).then_inc(silu_done, 1)
            norm_stats(0, XC)
            act.activation(SP[:, 0:1], vec("alpha"), ACT.Abs).then_inc(sp_done, 1)
            act.wait_ge(sp_done, 1)
            act.activation(SP[:, 1:2], SP[:, 0:1], ACT.Exp, scale=-1.0).then_inc(sp_done, 1)
            act.wait_ge(sp_done, 2)
            act.wait_ge(const_done, 4)
            act.activation(SP[:, 2:3], SP[:, 1:2], ACT.Ln, bias=CON[:, 2:3]).then_inc(sp_done, 1)
            for t in range(NBLK):
                act.wait_ge(kd_done, t + 1)
                act.activation(LAT[:, t * BLK:(t + 1) * BLK], PS[0:64, t, :], ACT.Gelu, bias=vec("bkd")[0:64, :])\
                   .then_inc(lat_done, 1)

            def evac_proj(n, g):
                act.wait_ge(proj_done, n + 1)
                if not (isinstance(n, int) and n == 0):
                    act.wait_ge(qx_ready, 2 * n)
                act.activation(QT[:, :], PS[:, 6, 0:256], ACT.Identity, bias=vec("bq", g)).then_inc(qk_evac, 1)
                act.activation(KT[:, :], PS[:, 6, 256:512], ACT.Identity, bias=vec("bk", g)).then_inc(qk_evac, 1)
                act.wait_ge(qk_evac, 4 * n + 2)
                act.activation(QR, QT[:, :], ACT.Copy, scale=vec("q_sign")).then_inc(qk_evac, 1)
                act.activation(KR, KT[:, :], ACT.Copy, scale=vec("k_sign")).then_inc(qk_evac, 1)

            def exps(n, n0):
                for h in range(2):
                    act.wait_ge(st_done, 2 * n + h + 1)
                    if n0 >= 2:
                        act.wait_ge(pv_done, n - 1)
                    for out in (PR, PH)[:2 - h]:
                        act.activation(out[:, n0 % 2, 2 * h:2 * h + 2, :], PS[:, 2 + 2 * h:4 + 2 * h, 0:384],
                                       ACT.Exp, scale=SCALE).then_inc(exp_done, 1)

            def evac_out(n, n0):
                act.wait_ge(pv_done, n + 1)
                if n0 >= 2:
                    act.wait_ge(on_done, n - 1)
                act.activation(OT[:, n0 % 2, :], PS[:, 7, 0:256], ACT.Copy).then_inc(ot_done, 1)

            def recip(n, n0):
                act.wait_ge(su_done, n + 1)
                act.activation(SU[:, n0 % 2, :], SU[:, n0 % 2, :], ACT.Ln).then_inc(ls_done, 1)
                act.wait_ge(ls_done, n + 1)
                act.activation(SU[:, n0 % 2, :], SU[:, n0 % 2, :], ACT.Exp, scale=-1.0).then_inc(rsx_done, 1)

            def step(n0, it=0):
                n = n0 + 8 * it
                if n0 >= 2:
                    evac_out(n - 2, n0 - 2)
                exps(n, n0)
                if n0 + 3 < UNITS:
                    evac_proj(n + 3, (n0 + 3) % 4)
                if n0 >= 2:
                    recip(n - 2, n0 - 2)

            act.preload_act_table_set("natural_log_exp_and_others")
            evac_proj(0, 0)
            evac_proj(1, 1)
            evac_proj(2, 2)
            for n in range(4):
                step(n)
            with act.Fori(0, 3) as it:
                for u in range(8):
                    step(4 + u, it)
            for n in range(28, UNITS):
                step(n)
            evac_out(30, 30)
            recip(30, 30)
            square(1, XC, 0)
            square(1, XC, 1)
            evac_out(31, 31)
            recip(31, 31)
            inverse(1, 0)
            square(1, XC, 2)
            inverse(1, 1)
            inverse(1, 2)
            square(1, XC, 3)
            inverse(1, 3)

            router_exp(0)
            s = moe[0]

            def gelus(m, m0, e):
                for c in range(4):
                    act.wait_ge(s["h"], 4 * m + c + 1)
                    if m0 >= 1:
                        act.wait_ge(s["lo"], 4 * m - 4 + c + 1)
                    if m0 >= 2:
                        act.wait_ge(s["y"], m - 1)
                    if m0 % 4 == 0 and c == 0:
                        act.wait_ge(bias_done, e + 1)
                    bias = BI[:, m0 // 4 % 2, c:c + 1]
                    act.activation(G[:, c, :], PS[:, c, :], ACT.Gelu_apprx_tanh, bias=bias).then_inc(s["act"], 1)
                    act.activation(GH[:, m0 % 2, c, :], PS[:, c, :], ACT.Gelu_apprx_tanh, bias=bias)\
                       .then_inc(s["act"], 1)
                    if m0 % 4 == 3 and c == 0 and m0 < 35:
                        act.activation(BI[:, (m0 // 4 + 1) % 2, :], V[:, bass.ds(VAT["b1"] + 4 * e + 4, 4)],
                                       ACT.Copy).then_inc(bias_done, 1)

            act.activation(BI[:, 0, :], V[:, VAT["b1"]:VAT["b1"] + 4], ACT.Copy).then_inc(bias_done, 1)
            for m in range(8):
                gelus(m, m, m // 4)
            with act.Fori(1, 4) as it:
                for u in range(8):
                    gelus(8 * it + u, 8 + u, 2 * it + u // 4)
            for m in range(32, 36):
                gelus(m, m, 8)

            act.preload_act_table_set("natural_log_exp_and_others")
            square(2, XC, 0)
            square(2, XC, 1)
            inverse(2, 0)
            inverse(2, 1)
            square(3, HN, 0)
            square(2, XC, 2)
            inverse(3, 0)
            square(3, HN, 1)
            inverse(2, 2)
            square(2, XC, 3)
            inverse(3, 1)
            inverse(2, 3)
            for t in (2, 3):
                square(3, HN, t)
                inverse(3, t)
            for i, (p, t) in enumerate(projected):
                if p == 3:
                    continue
                act.wait_ge(p1_psum, i + 1)
                func = (ACT.Sigmoid, ACT.Sigmoid, ACT.Gelu)[p]
                act.activation(blk((R_, I_, GATE)[p], t), PS[:, i % 8, :], func, bias=vec("pb", p))\
                   .then_inc(p1_done, 1)
            act.preload_act_table_set("natural_log_exp_and_others")
            act.wait_ge(sp_done, 5)
            for t in range(NBLK):
                act.wait_ge(p1_done, evacuated(projected.index((0, t))))
                act.activation(blk(A_, t), blk(R_, t), ACT.Exp, scale=SP[:, 3:4]).then_inc(a_done, 1)

            def root(t):
                act.wait_ge(sa_done, 2 * t + 2)
                act.activation(blk(SA, t), blk(SA, t), ACT.Ln).then_inc(ln_done, 1)
                act.wait_ge(ln_done, t + 1)
                act.activation(blk(SA, t), blk(SA, t), ACT.Exp, scale=0.5).then_inc(sqrt_done, 1)

            root(0)
            root(1)
            square(4, H2, 0)
            root(2)
            inverse(4, 0)
            square(4, H2, 1)
            root(3)
            inverse(4, 1)
            for t in (2, 3):
                square(4, H2, t)
                inverse(4, t)
            act.preload_act_table_set("gelu_and_others")
            for t in range(NBLK):
                for c in range(3):
                    i = 3 * t + c
                    act.wait_ge(mlp_psum, i + 1)
                    if t >= 1:
                        act.wait_ge(pf_done, i - 2)
                    act.activation(GG[:, c, :], PS[:, c, :], ACT.Gelu, bias=vec("gb", c)).then_inc(gg_done, 1)

            act.preload_act_table_set("natural_log_exp_and_others")
            square(5, XC, 0)
            square(5, XC, 1)
            inverse(5, 0)
            square(5, XC, 2)
            inverse(5, 1)
            square(5, XC, 3)
            inverse(5, 2)
            inverse(5, 3)
            router_exp(1)
            s1 = moe[1]

            def silus(m, m0):
                for c in range(2):
                    act.wait_ge(s1["h"], 2 * m + c + 1)
                    if m0 >= 1:
                        act.wait_ge(s1["prod"], 2 * m - 2 + c + 1)
                    act.activation(SG[:, c, :], PS[:, c, :], ACT.Silu).then_inc(s1["act"], 1)
                    act.wait_ge(s1["prod"], 2 * m + c + 1)
                    if m0 >= 2:
                        act.wait_ge(s1["y"], m - 1)
                    act.activation(GH[:, m0 % 2, c, :], G[:, c, :], ACT.Copy).then_inc(s1["gh"], 1)

            for m in range(8):
                silus(m, m)
            with act.Fori(1, 4) as it:
                for u in range(8):
                    silus(8 * it + u, 8 + u)

        @block.vector
        def _(dve):
            def centre(k, t):
                dve.wait_ge(mean_done, 4 * centred(k) + t + 1)
                dve.tensor_tensor(out=blk(XC, t), in0=blk(X, t), in1=PS[:, t, :], op=ALU.subtract)\
                   .then_inc(cen_done, 1)

            def normalise(k, t):
                layer, which = k // 2 if k < 5 else 1, {0: 0, 1: 1, 2: 0, 5: 1}[k]
                dve.wait_ge(rstd_done, norm_at(k, t) + 1)
                dve.tensor_tensor(out=blk(HN, t), in0=blk(XC, t), in1=blk(STAT, t), op=ALU.mult)\
                   .then_inc(nrm_done, 1)
                dve.wait_ge(nrm_done, norm_at(k, t) + 1)
                for b in (2 * t, 2 * t + 1):
                    dve.tensor_scalar(blk(HN, b, SEQ), blk(HN, b, SEQ), MC[:, layer, which, b:b + 1],
                                      MOD[:, layer, 3 * which, b:b + 1], ALU.mult, ALU.add)\
                       .then_inc(hn_done, 1)

            def rms(k, src, weight, t):
                dve.wait_ge(rstd_done, norm_at(k, t) + 1)
                dve.scalar_tensor_tensor(out=blk(XC, t), in0=blk(src, t), scalar=vec(weight),
                                         in1=blk(STAT, t), op0=ALU.mult, op1=ALU.mult)\
                   .then_inc(nrm_done, 1)

            def rest(k, src, t):
                dve.wait_ge(hh_done, 4 * split_at(k) + t + 1)
                dve.tensor_tensor(out=blk(HL, t), in0=blk(src, t), in1=f(blk(HH, t)), op=ALU.subtract)\
                   .then_inc(hl_done, 1)

            def residual_acc(n, s, ne, t):
                dve.wait_ge(s["acc"], 4 * ne - 3 + t)
                for b in (2 * t, 2 * t + 1):
                    ins = dve.scalar_tensor_tensor(out=blk(X, b, SEQ), in0=blk(ACC, b, SEQ),
                                                   scalar=MG[:, n, 1, b:b + 1], in1=blk(X, b, SEQ),
                                                   op0=ALU.mult, op1=ALU.add)
                ins.then_inc(x_upd, 1)

            def route(n, ne):
                s = moe[n]
                count = [0]
                lg, e, k1, k2, e2, w = (RT[k][:, :, :] for k in ("lg", "e", "k1", "k2", "e2", "w"))
                m, m1, km1, m2, km2, den = (RM[k][:, :] for k in ("m", "m1", "km1", "m2", "km2", "den"))
                prio = V[:, VAT["prio"]:VAT["prio"] + 8].unsqueeze(1).to_broadcast([128, 16, 8])

                def each(x):
                    return x.unsqueeze(2).to_broadcast([128, 16, 8])

                def link(ins, name="rstep"):
                    count[0] += name == "rstep"
                    ins.then_inc(s[name], 1)
                    if name == "rstep":
                        dve.wait_ge(s[name], count[0])

                dve.wait_ge(s["logits"], 1)
                lp = PS[:, 7, 0:128].rearrange("p (i e) -> p i e", e=8)
                if n == 0:
                    rb = ROWS[:, 128:136].unsqueeze(1).to_broadcast([128, 16, 8])
                    dve.wait_ge(in_rows, 32)
                    dve.tensor_tensor(out=lg, in0=lp, in1=rb, op=ALU.add).then_inc(s["lg"], 1)
                else:
                    dve.tensor_copy(lg, lp).then_inc(s["lg"], 1)
                dve.wait_ge(s["lg"], 1)
                dve.tensor_reduce(m, lg, axis=AX.X, op=ALU.max).then_inc(s["lg"], 1)
                dve.wait_ge(s["lg"], 2)
                dve.tensor_tensor(out=lg, in0=lg, in1=each(m), op=ALU.subtract).then_inc(s["lg"], 1)
                dve.wait_ge(s["exps"], 1)
                link(dve.tensor_reduce(m1, e, axis=AX.X, op=ALU.max))
                link(dve.tensor_tensor(out=k1, in0=e, in1=each(m1), op=ALU.is_equal))
                link(dve.tensor_tensor(out=k1, in0=k1, in1=prio, op=ALU.mult))
                link(dve.tensor_reduce(km1, k1, axis=AX.X, op=ALU.max))
                link(dve.tensor_tensor(out=k1, in0=k1, in1=each(km1), op=ALU.is_equal))
                link(dve.scalar_tensor_tensor(out=e2, in0=k1, scalar=-2.0, in1=e, op0=ALU.mult, op1=ALU.add))
                link(dve.tensor_reduce(m2, e2, axis=AX.X, op=ALU.max))
                link(dve.tensor_tensor(out=k2, in0=e2, in1=each(m2), op=ALU.is_equal))
                link(dve.tensor_tensor(out=k2, in0=k2, in1=prio, op=ALU.mult))
                link(dve.tensor_reduce(km2, k2, axis=AX.X, op=ALU.max))
                link(dve.tensor_tensor(out=k2, in0=k2, in1=each(km2), op=ALU.is_equal))
                link(dve.tensor_tensor(out=k1, in0=k1, in1=k2, op=ALU.add))
                link(dve.tensor_tensor(out=w, in0=k1, in1=e, op=ALU.mult))
                link(dve.tensor_tensor(out=den, in0=m1, in1=m2, op=ALU.add))
                link(dve.reciprocal(den, den))
                dve.tensor_tensor(out=COMB[:, :, 0:8], in0=w, in1=each(den), op=ALU.mult).then_inc(s["comb"], 1)
                if ne == 9:
                    dve.memset(COMB[:, :, 8:9], 1.0).then_inc(s["comb"], 1)

            def routes_in(n, ne):
                s = moe[n]
                for t in range(NBLK):
                    dve.wait_ge(s["combT"], t + 1)
                    dve.tensor_copy(CT[0:ne, t * BLK:(t + 1) * BLK], PS[0:ne, 6 + t % 2, :]).then_inc(s["ct"], 1)

            def moe_scale(s, m, m0, pair):
                slot = m0 // 4 % 2
                dve.wait_ge(s["y"], m + 1)
                dve.wait_ge(s[f"wb_in{slot}"], 16 * (pair + 1))
                if m0 >= 2:
                    dve.wait_ge(s["acc"], m - 1)
                t = m0 % 4
                dve.tensor_tensor(out=YW[:, m0 % 2, :], in0=PS[:, 4 + m0 % 4, :],
                                  in1=WB[:, slot, t * BLK:(t + 1) * BLK], op=ALU.mult).then_inc(s["ymul"], 1)

            for t in range(NBLK):
                centre(0, t)

            dve.wait_ge(mod_psum, 1)
            mp = PS[:, 7, 0:96].rearrange("p (l i b) -> p l i b", l=2, i=6)
            dve.tensor_copy(MOD[:, :, :, :], mp).then_inc(mod_done, 1)
            dve.tensor_scalar(MC[:, :, :, :], mp[:, :, 1::3, :], 1.0, None, ALU.add).then_inc(mod_done, 1)
            dve.wait_ge(mod_done, 2)
            gates = MOD[:, :, 2::3, :]
            dve.tensor_scalar(GS[:, :, :, :], gates, 0.0, 2.0, ALU.is_ge, ALU.mult).then_inc(gate_done, 1)
            for layer in range(2):
                dve.scalar_tensor_tensor(out=GA[:, layer, :, :], in0=gates[:, layer, :, :], scalar=-1.0,
                                         in1=gates[:, layer, :, :], op0=ALU.mult, op1=ALU.max)\
                   .then_inc(gate_done, 1)
            dve.wait_ge(gate_done, 3)
            dve.tensor_scalar(GA[:, :, :, :], GA[:, :, :, :], 0.25, None, ALU.max).then_inc(gate_done, 1)
            dve.wait_ge(gate_done, 4)
            dve.scalar_tensor_tensor(out=MG[:, :, :, :].rearrange("p l w b -> p (l w b)"),
                                     in0=GS[:, :, :, :].rearrange("p l w b -> p (l w b)"), scalar=-1.0,
                                     in1=GA[:, :, :, :].rearrange("p l w b -> p (l w b)"),
                                     op0=ALU.add, op1=ALU.mult).then_inc(gate_done, 1)
            for t in range(NBLK):
                normalise(0, t)
            def all_values(j):
                dve.wait_ge(v_psum, j + 1)
                dve.tensor_tensor(out=VALL[:, 4 * j:4 * j + 4, :],
                                  in0=PS[:, 2 + j, :].rearrange("p (i c) -> p i c", i=4),
                                  in1=ROWS[:, 0:128].unsqueeze(1).to_broadcast([128, 4, 128]), op=ALU.add)\
                   .then_inc(vall_done, 1)

            def join(n, g):
                dve.wait_ge(qk_evac, 4 * n + 4)
                if not isinstance(n, int) or n >= 4:
                    dve.wait_ge(st_done, 2 * n - 6)
                dve.scalar_tensor_tensor(out=QX[:, g, :], in0=QT[:, :], scalar=vec("q_keep"), in1=f(QR),
                                         op0=ALU.mult, op1=ALU.add).then_inc(qx_ready, 1)
                dve.scalar_tensor_tensor(out=KX[:, g, :], in0=KT[:, :], scalar=vec("k_keep"), in1=f(KR),
                                         op0=ALU.mult, op1=ALU.add).then_inc(qx_ready, 1)

            nmv = NM[:, :].rearrange("p (q j) -> p q j", q=2)

            def maxima(n, n0, h):
                dve.wait_ge(s_done, 2 * n + h + 1)
                if h == 0 and n0 >= 1:
                    dve.wait_ge(mp_ready, 2 * n)
                for q, keys in enumerate((slice(0, 128), slice(128, 384))):
                    dve.tensor_reduce(nmv[:, q, 2 * h:2 * h + 2], PS[:, 0:2, keys], axis=AX.X, op=ALU.max,
                                      negate=True).then_inc(max_done, 1)

            def spread_max(n, n0):
                dve.wait_ge(max_done, 4 * n + 4)
                dve.tensor_copy(NMH, NM[:, :]).then_inc(nmh_done, 1)
                dve.wait_ge(nmh_done, n + 1)
                if n0 >= 1:
                    dve.wait_ge(mt_done, n)
                dve.tensor_copy(MP[:, :, 24::32], f(NMH).rearrange("p (q j) -> p q j", q=2)).then_inc(mp_ready, 1)
                dve.tensor_tensor(out=MP[:, :, 25::32], in0=nmv, in1=f(NMH).rearrange("p (q j) -> p q j", q=2),
                                  op=ALU.subtract).then_inc(mp_ready, 1)

            def with_max(n, n0):
                dve.wait_ge(mt_done, n + 1)
                if n0 >= 2:
                    dve.wait_ge(st_done, 2 * n - 2)
                dve.tensor_tensor(out=QM[:, n0 % 2, :], in0=f(QX[:, n0 % 4, :]), in1=PS[:, 7, 256:512], op=ALU.add)\
                   .then_inc(qm_ready, 1)

            def spread_sum(n, n0):
                if n0 == 0:
                    dve.wait_ge(ot_done, n + 1)
                dve.stream_shuffle(SU[:, n0 % 2, :], OT[:, n0 % 2, :], [16] * 32).then_inc(su_done, 1)

            def divide(n, n0, it):
                dve.wait_ge(rsx_done, n + 1)
                if n0 + 1 < UNITS:
                    dve.wait_ge(ot_done, n + 2)
                if n0 >= 1:
                    dve.wait_ge(on_done, n)
                dve.tensor_tensor(out=ON[:, n0 % 4, bass.ds((2 * it + n0 // 4) * SEQ, SEQ)],
                                  in0=OT[:, n0 % 2, :], in1=SU[:, n0 % 2, :], op=ALU.mult).then_inc(on_done, 1)

            def place_values(b, b0):
                if b0 >= 1:
                    dve.wait_ge(pv_done, 4 * b)
                for kt in range(2):
                    own = VALL[:, bass.ds(2 * b + kt, 1), :].rearrange("p a (h c) -> p (a h) c", c=8)
                    dve.tensor_copy(values_of(kt, 0, 8), own).then_inc(vx_ready, 1)
                dve.wait_ge(vx_ready, 4 * b + 2)
                for kt in range(2):
                    own = VALL[:, bass.ds(2 * b + kt, 1), :].rearrange("p a (h c) -> p (a h) c", c=8)
                    dve.tensor_tensor(out=values_of(kt, 8, 16), in0=own, in1=f(values_of(kt, 0, 8)),
                                      op=ALU.subtract).then_inc(vx_ready, 1)

            def upper(n, n0):
                dve.wait_ge(exp_done, 3 * n + 3)
                if n0 >= 2:
                    dve.wait_ge(pv_done, n - 1)
                dve.tensor_copy(PH[:, n0 % 2, 2:4, :], PR[:, n0 % 2, 2:4, :]).then_inc(hi_done, 1)

            def attended(t):
                dve.wait_ge(wo_done, t + 1)
                for b in (2 * t, 2 * t + 1):
                    dve.tensor_scalar(blk(XC, b, SEQ), PS[:, 6, (b % 2) * SEQ:(b % 2 + 1) * SEQ], vec("bo"),
                                      MG[:, 0, 0, b:b + 1], ALU.add, ALU.mult).then_inc(y_scaled, 1)
                dve.wait_ge(y_scaled, 2 * t + 2)
                dve.tensor_tensor(out=blk(X, t), in0=blk(X, t), in1=blk(XC, t), op=ALU.add).then_inc(x_upd, 1)

            def step(n0, it=0):
                n = n0 + 8 * it
                if n0 % 4 == 1 and n0 > 1:
                    place_values(2 * it + n0 // 4, n0 // 4)
                if n0 + 1 < UNITS:
                    maxima(n + 1, n0 + 1, 1)
                    spread_max(n + 1, n0 + 1)
                if n0 >= 3:
                    divide(n - 3, n0 - 3, it)
                if n0 >= 2:
                    spread_sum(n - 2, n0 - 2)
                if n0 + 1 < UNITS:
                    with_max(n + 1, n0 + 1)
                if n0 + 2 < UNITS:
                    maxima(n + 2, n0 + 2, 0)
                upper(n, n0)
                if n0 + 3 < UNITS:
                    join(n + 3, (n0 + 3) % 4)
                else:
                    attended(n0 - 29)

            dve.wait_ge(sp_done, 3)
            dve.scalar_tensor_tensor(out=SP[:, 3:4], in0=vec("alpha"), scalar=0.0, in1=SP[:, 2:3],
                                     op0=ALU.max, op1=ALU.add).then_inc(sp_done, 1)
            dve.wait_ge(sp_done, 4)
            dve.tensor_scalar(SP[:, 3:4], SP[:, 3:4], -8.0, None, ALU.mult).then_inc(sp_done, 1)
            dve.wait_ge(ident_done, 9)
            dve.wait_ge(in_rows, 32)
            join(0, 0)
            all_values(0)
            all_values(1)
            maxima(0, 0, 0)
            all_values(2)
            maxima(0, 0, 1)
            spread_max(0, 0)
            join(1, 1)
            with_max(0, 0)
            all_values(3)
            dve.wait_ge(ones_done, 4)
            dve.wait_ge(vall_done, 4)
            place_values(0, 0)
            maxima(1, 1, 0)
            join(2, 2)
            for n in range(4):
                step(n)
            with dve.Fori(0, 3) as it:
                for u in range(8):
                    step(4 + u, it)
            for n in range(28, UNITS):
                step(n)
            divide(29, 29, 0)
            spread_sum(30, 30)
            centre(1, 0)
            centre(1, 1)
            divide(30, 30, 0)
            spread_sum(31, 31)
            centre(1, 2)
            divide(31, 31, 0)
            normalise(1, 0)
            normalise(1, 1)
            attended(3)
            normalise(1, 2)
            rest(1, HN, 0)
            rest(1, HN, 1)
            centre(1, 3)
            rest(1, HN, 2)
            normalise(1, 3)
            rest(1, HN, 3)

            route(0, E0)
            s = moe[0]
            routes_in(0, E0)

            def bias_sum(t):
                dve.wait_ge(s["b2_psum"], t + 1)
                dve.tensor_copy(blk(ACC, t), PS[:, 6 + t % 2, :]).then_inc(s["acc_init"], 1)

            def lower0(m, m0):
                for c in range(4):
                    dve.wait_ge(s["act"], 2 * (4 * m + c + 1))
                    if m0 >= 2:
                        dve.wait_ge(s["y"], m - 1)
                    dve.tensor_tensor(out=GL[:, m0 % 2, c, :], in0=G[:, c, :], in1=f(GH[:, m0 % 2, c, :]),
                                      op=ALU.subtract).then_inc(s["lo"], 1)

            dve.wait_ge(s["lo"], 4)
            lower0(1, 1)
            for t in range(NBLK):
                bias_sum(t)
            lower0(2, 2)
            for m in range(2, 8):
                lower0(m + 1, m + 1)
                moe_scale(s, m - 2, m - 2, 0)
            with dve.Fori(1, 4) as it:
                for u in range(8):
                    lower0(8 * it + u + 1, 9 + u)
                    moe_scale(s, 8 * it + u - 2, 6 + u, it - (u < 2))
            lower0(33, 33)
            moe_scale(s, 30, 30, 3)
            lower0(34, 34)
            moe_scale(s, 31, 31, 3)
            moe_scale(s, 32, 32, 4)
            lower0(35, 35)
            moe_scale(s, 33, 33, 4)
            moe_scale(s, 34, 34, 4)

            residual_acc(0, s, E0, 0)
            residual_acc(0, s, E0, 1)
            centre(2, 0)
            centre(2, 1)
            moe_scale(s, 35, 35, 4)
            normalise(2, 0)
            residual_acc(0, s, E0, 2)
            residual_acc(0, s, E0, 3)
            normalise(2, 1)
            centre(2, 2)
            centre(2, 3)
            rms(3, HN, "norm", 0)
            normalise(2, 2)
            rest(3, XC, 0)
            rms(3, HN, "norm", 1)
            normalise(2, 3)
            rest(3, XC, 1)
            rms(3, HN, "norm", 2)
            rest(3, XC, 2)
            rms(3, HN, "norm", 3)
            rest(3, XC, 3)
            for t in range(NBLK):
                i = projected.index((3, t))
                dve.wait_ge(p1_psum, i + 1)
                dve.wait_ge(p1_done, evacuated(i))
                dve.scalar_tensor_tensor(out=blk(HS, t), in0=PS[:, i % 8, :], scalar=vec("pb", 3),
                                         in1=blk(I_, t), op0=ALU.add, op1=ALU.mult).then_inc(hsi_done, 1)

            def one_less_square(t):
                dve.wait_ge(a_done, t + 1)
                dve.scalar_tensor_tensor(out=blk(SA, t), in0=blk(A_, t), scalar=-1.0, in1=blk(A_, t),
                                         op0=ALU.mult, op1=ALU.mult).then_inc(sa_done, 1)
                dve.wait_ge(sa_done, 2 * t + 1)
                dve.tensor_scalar(blk(SA, t), blk(SA, t), 1.0, 1e-37, ALU.add, ALU.max).then_inc(sa_done, 1)

            def recurrence(t):
                dve.wait_ge(hsi_done, t + 1)
                dve.wait_ge(sqrt_done, t + 1)
                dve.tensor_tensor(out=blk(HS, t), in0=blk(HS, t), in1=blk(SA, t), op=ALU.mult).then_inc(s_ready, 1)
                dve.wait_ge(s_ready, t + 1)
                for b in (2 * t, 2 * t + 1):
                    dve.tensor_tensor_scan(out=blk(I_, b, SEQ), data0=blk(A_, b, SEQ), data1=blk(HS, b, SEQ),
                                           initial=0.0, op0=ALU.mult, op1=ALU.add).then_inc(scan_done, 1)
                dve.wait_ge(scan_done, 2 * t + 2)
                dve.wait_ge(p1_done, 8 + t + 1)
                dve.tensor_tensor(out=blk(H2, t), in0=blk(I_, t), in1=blk(GATE, t), op=ALU.mult).then_inc(hs2_mul, 1)
                dve.wait_ge(hs2_mul, t + 1)
                dve.tensor_tensor(out=blk(H2, t), in0=blk(H2, t), in1=blk(HN, t), op=ALU.add).then_inc(hs2_done, 1)

            one_less_square(0)
            one_less_square(1)
            recurrence(0)
            one_less_square(2)
            recurrence(1)
            one_less_square(3)
            rms(4, H2, "norm2", 0)
            recurrence(2)
            rest(4, XC, 0)
            rms(4, H2, "norm2", 1)
            recurrence(3)
            rest(4, XC, 1)
            rms(4, H2, "norm2", 2)
            rest(4, XC, 2)
            rms(4, H2, "norm2", 3)
            rest(4, XC, 3)

            def mlp_mid(t):
                for c in range(3):
                    i = 3 * t + c
                    dve.wait_ge(gg_done, i + 1)
                    if t >= 1:
                        dve.wait_ge(pl_done, i - 2)
                    dve.scalar_tensor_tensor(out=PF[:, c, :], in0=PS[:, 3 + c, :], scalar=vec("fb", c),
                                             in1=GG[:, c, :], op0=ALU.add, op1=ALU.mult).then_inc(pf_done, 1)
                for c in range(3):
                    i = 3 * t + c
                    dve.wait_ge(ph_done, i + 1)
                    dve.tensor_tensor(out=GL[:, t % 2, c, :], in0=PF[:, c, :], in1=f(GH[:, t % 2, c, :]),
                                      op=ALU.subtract).then_inc(pl_done, 1)

            def mlp_out(t):
                dve.wait_ge(z_psum, t + 1)
                dve.scalar_tensor_tensor(out=blk(XC, t), in0=PS[:, 6 + t % 2, :], scalar=vec("outb"),
                                         in1=blk(H2, t), op0=ALU.add, op1=ALU.add).then_inc(z_done, 1)
                dve.wait_ge(z_done, t + 1)
                for b in (2 * t, 2 * t + 1):
                    ins = dve.scalar_tensor_tensor(out=blk(X, b, SEQ), in0=blk(XC, b, SEQ),
                                                   scalar=MG[:, 1, 0, b:b + 1], in1=blk(X, b, SEQ),
                                                   op0=ALU.mult, op1=ALU.add)
                ins.then_inc(x_upd, 1)

            mlp_mid(0)
            for t in range(3):
                mlp_mid(t + 1)
                mlp_out(t)

            centre(5, 0)
            centre(5, 1)
            mlp_out(3)
            centre(5, 2)
            normalise(5, 0)
            centre(5, 3)
            normalise(5, 1)
            rest(5, HN, 0)
            normalise(5, 2)
            rest(5, HN, 1)
            normalise(5, 3)
            rest(5, HN, 2)
            rest(5, HN, 3)
            route(1, E1)
            routes_in(1, E1)
            s1 = moe[1]

            def middle1(m, m0, meanwhile=None):
                for c in range(2):
                    dve.wait_ge(s1["act"], 2 * m + c + 1)
                    if m0 >= 1:
                        dve.wait_ge(s1["lo"], 2 * m - 2 + c + 1)
                    dve.tensor_tensor(out=G[:, c, :], in0=PS[:, 2 + c, :], in1=SG[:, c, :], op=ALU.mult)\
                       .then_inc(s1["prod"], 1)
                    if c == 1 and meanwhile:
                        meanwhile()
                    dve.wait_ge(s1["gh"], 2 * m + c + 1)
                    if m0 >= 2:
                        dve.wait_ge(s1["y"], m - 1)
                    dve.tensor_tensor(out=GL[:, m0 % 2, c, :], in0=G[:, c, :], in1=f(GH[:, m0 % 2, c, :]),
                                      op=ALU.subtract).then_inc(s1["lo"], 1)

            for m in range(3):
                middle1(m, m)
            for m in range(2, 8):
                middle1(m + 1, m + 1, lambda: moe_scale(s1, m - 2, m - 2, 0))
            with dve.Fori(1, 3) as it:
                for u in range(8):
                    middle1(8 * it + u + 1, 9 + u,
                            lambda: moe_scale(s1, 8 * it + u - 2, 6 + u, it - (u < 2)))
            for m in range(24, 31):
                middle1(m + 1, m + 1, lambda: moe_scale(s1, m - 2, m - 2, (m - 2) // 8))
            for m in (29, 30, 31):
                moe_scale(s1, m, m, 3)
            for t in range(NBLK):
                residual_acc(1, s1, E1, t)

        @block.tensor
        def _(pe):
            def three(out, wh, wl, xh, xl, first, last):
                pe.matmul(out, wh, xh, start=first, stop=False)
                pe.matmul(out, wl, xh, start=False, stop=False)
                return pe.matmul(out, wh, xl, start=False, stop=last)

            def mean(k, t):
                if k == 0:
                    pe.wait_ge(in_x[t], 16)
                else:
                    pe.wait_ge(x_upd, 4 * centred(k) + t - 3)
                if k == 1 and t == 0:
                    pe.wait_ge(max_done, 4 * UNITS)
                elif k == 1 and t == 2:
                    pe.wait_ge(exp_done, 3 * UNITS - 1)
                pe.matmul(PS[:, t, :], OND[:, :], blk(X, t), start=True, stop=True).then_inc(mean_done, 1)

            def variance(k, t):
                at = norm_at(k, t)
                pe.wait_ge(sq_done, at + 1)
                if k == 1 and t == 0:
                    pe.wait_ge(exp_done, 3 * UNITS)
                if at >= 2:
                    pe.wait_ge(lnv_done, at - 1)
                pe.matmul(PS[:, variance_bank(k, t), :], OND[:, :], blk(STAT, t), start=True, stop=True)\
                  .then_inc(var_done, 1)

            def router(n, t):
                name = ("router", "wg")[n]
                pe.wait_ge(hn_done, 8 * centred((1, 5)[n]) + 2 * t + 2)
                for i in range(4 * t, 4 * t + 4):
                    mm = pe.matmul(PS[:, 7, 8 * i:8 * i + 8], HN[:, 128 * i:128 * i + 128], mat(name, 0, 8),
                                   start=True, stop=True)
                if t == 3:
                    mm.then_inc(moe[n]["logits"], 1)

            def route_out(n, ne, t):
                s = moe[n]
                if t == 0:
                    pe.wait_ge(s["comb"], 2 if ne == 9 else 1)
                if t >= 2:
                    pe.wait_ge(s["ct"], t - 1)
                for i in range(4 * t, 4 * t + 4):
                    mm = pe.transpose(PS[0:ne, 6 + t % 2, 128 * (i % 4):128 * (i % 4) + 128], COMB[:, i, 0:ne],
                                      IDF[:, :])
                mm.then_inc(s["combT"], 1)

            pe.wait_ge(const_done, 4)
            for _ in range(7):
                pe.matmul(PS[:, 7, 0:128], OND[:, :], OND[:, :], start=True, stop=True)
            for t in range(NBLK):
                mean(0, t)
            variance(0, 0)
            variance(0, 1)
            pe.wait_ge(in_mod, 16)
            pe.wait_ge(silu_done, 1)
            for layer in range(2):
                for i in range(6):
                    mm = pe.matmul(PS[:, 7, 48 * layer + 8 * i:48 * layer + 8 * i + 8],
                                   WMOD[:, 768 * layer + 128 * i:768 * layer + 128 * i + 128],
                                   SC[:, 8 * layer:8 * layer + 8], start=True, stop=True)
            mm.then_inc(mod_psum, 1)
            variance(0, 2)
            variance(0, 3)
            pe.wait_ge(in_mats, 16)
            for t in range(NBLK):
                pe.wait_ge(hn_done, 2 * t + 2)
                pe.matmul(PS[0:64, t, :], mat("wkd", 0, 64), blk(HN, t), start=True, stop=True)\
                  .then_inc(kd_done, 1)
            def project(n, n0, it):
                g, cols = n0 % 4, bass.ds((2 * it + n0 // 4) * SEQ, SEQ)
                if n0 >= 1:
                    pe.wait_ge(qk_evac, 4 * n)
                pe.matmul(PS[:, 6, 0:256], mat("wq", g), HN[:, cols], start=True, stop=True)
                pe.matmul(PS[:, 6, 256:512], KM[:, 128 * g:128 * g + 128], LAT[:, cols], start=True, stop=True)\
                  .then_inc(proj_done, 1)

            def diagonal(bank):
                return PS[:, bank, :].rearrange("p (a b) -> p a b", b=256)[:, :, 0:128]

            def mask(m):
                return m[:, :].unsqueeze(1).to_broadcast([128, 2, 128])

            def scores(n, n0, h):
                g = n0 % 4
                if h == 0:
                    pe.wait_ge(qx_ready, 2 * n + 2)
                    if n0 >= 1:
                        pe.wait_ge(max_done, 4 * n)
                else:
                    pe.wait_ge(max_done, 4 * n + 2)
                for j in range(2):
                    r = slice(64 * h + 32 * j, 64 * h + 32 * j + 32)
                    pe.matmul(PS[:, j, 0:128], QX[r, g, 0:128], KX[r, g, 0:128], start=True, stop=False)
                    pe.matmul(PS[:, j, 128:384], QX[r, g, 128:256], KX[r, g, :], start=False, stop=False)
                for j in range(2):
                    mm = pe.matmul(diagonal(j), IDB[:, :], mask(MKQ), start=False, stop=True)
                mm.then_inc(s_done, 1)

            def scores_t(n, n0, h):
                g = n0 % 4
                if h == 0:
                    pe.wait_ge(qm_ready, n + 1)
                if n0 >= 1:
                    pe.wait_ge(exp_done, 3 * n - 1 + h)
                for j in range(2):
                    r = slice(64 * h + 32 * j, 64 * h + 32 * j + 32)
                    bank = 2 + 2 * h + j
                    pe.matmul(PS[:, bank, 0:256], KX[r, g, 0:128], QM[r, n0 % 2, :], start=True, stop=False)
                    pe.matmul(PS[:, bank, 256:384], KX[r, g, 128:256], QM[r, n0 % 2, 128:256],
                              start=False, stop=False)
                for j in range(2):
                    mm = pe.matmul(diagonal(2 + 2 * h + j), IDB[:, :], mask(MKK), start=False, stop=True)
                mm.then_inc(st_done, 1)

            def values(n, n0, it):
                pe.wait_ge(lower_done, 2 * n + 2)
                pe.wait_ge(vx_ready, 4 * (2 * it + n0 // 4) + 4)
                if n0 >= 1:
                    pe.wait_ge(ot_done, n)
                if n0 + 2 < UNITS:
                    pe.wait_ge(qm_ready, n + 3)
                for j in range(4):
                    at = 128 * (4 * (n0 % 4) + j) + 96 - 32 * j
                    for i, part in enumerate((PH[:, n0 % 2, j, :], lower_of(n0, j // 2)[:, j % 2, :])):
                        first, last = i == j == 0, i == 1 and j == 3
                        pe.matmul(PS[:, 7, 0:256], VX[0][:, at:at + 128], part[:, 0:256],
                                  start=first, stop=False)
                        mm = pe.matmul(PS[:, 7, 128:256], VX[1][:, at:at + 128], part[:, 256:384],
                                       start=False, stop=last)
                mm.then_inc(pv_done, 1)

            def out_proj(t):
                pe.wait_ge(on_done, 8 * t + 8)
                if t == 0:
                    pe.wait_ge(qk_evac, 4 * UNITS)
                else:
                    pe.wait_ge(y_scaled, 2 * t)
                for g in range(4):
                    mm = pe.matmul(PS[:, 6, :], mat("wo", g), ON[:, g, t * BLK:(t + 1) * BLK],
                                   start=(g == 0), stop=(g == 3))
                mm.then_inc(wo_done, 1)

            def maxima_t(n, n0):
                pe.wait_ge(mp_ready, 2 * n + 2)
                if n0 >= 3:
                    pe.wait_ge(ot_done, n - 2)
                for q in range(2):
                    mm = pe.transpose(PS[:, 7, 256 + 128 * q:384 + 128 * q], MP[:, q, :], IDF[:, :])
                mm.then_inc(mt_done, 1)

            def step(n0, it=0):
                n = n0 + 8 * it
                if n0 + 1 < UNITS:
                    scores(n + 1, n0 + 1, 1)
                scores_t(n, n0, 0)
                scores_t(n, n0, 1)
                if n0 + 3 < UNITS:
                    project(n + 3, n0 + 3, it)
                else:
                    out_proj(n0 - 29)
                if n0 + 1 < UNITS:
                    maxima_t(n + 1, n0 + 1)
                if n0 + 2 < UNITS:
                    scores(n + 2, n0 + 2, 0)
                if n0 >= 1:
                    values(n - 1, n0 - 1, it)

            def keep_clock(count, bank=7):
                for _ in range(count):
                    pe.matmul(PS[:, bank, :], LH[:, 0:128], LH[:, 0:512], start=True, stop=True)

            pe.wait_ge(in_k, 16)
            pe.wait_ge(lat_done, 1)
            project(0, 0, 0)
            pe.wait_ge(lat_done, 4)
            for i in range(16):
                mm = pe.matmul(PS[:, 2 + i // 4, 128 * (i % 4):128 * (i % 4) + 128],
                               LAT[:, 128 * i:128 * i + 128], KM[:, 512:640], start=True, stop=True)
                if i % 4 == 3:
                    mm.then_inc(v_psum, 1)
            pe.wait_ge(ident_done, 9)
            pe.wait_ge(mod_done, 2)
            pe.wait_ge(l1_split, 1)
            scores(0, 0, 0)
            project(1, 1, 0)
            scores(0, 0, 1)
            project(2, 2, 0)
            keep_clock(8)
            maxima_t(0, 0)
            scores(1, 1, 0)
            pe.wait_ge(vall_done, 4)
            pe.wait_ge(qm_ready, 1)
            keep_clock(6)
            step(0)
            pe.wait_ge(qm_ready, 2)
            keep_clock(4)
            for n in range(1, 4):
                step(n)
            with pe.Fori(0, 3) as it:
                for u in range(8):
                    step(4 + u, it)
            for n in range(28, UNITS):
                step(n)

            mean(1, 0)
            mean(1, 1)
            values(31, 31, 0)
            mean(1, 2)
            variance(1, 0)
            variance(1, 1)
            out_proj(3)
            variance(1, 2)
            pe.wait_ge(ot_done, UNITS)
            router(0, 0)
            router(0, 1)
            mean(1, 3)
            router(0, 2)
            variance(1, 3)
            router(0, 3)

            s = moe[0]

            def bias_out(t):
                pe.wait_ge(s["ct"], 4)
                if t >= 2:
                    pe.wait_ge(s["acc_init"], t - 1)
                pe.matmul(PS[:, 6 + t % 2, :], B2[:, :], CT[0:E0, t * BLK:(t + 1) * BLK], start=True, stop=True)\
                  .then_inc(s["b2_psum"], 1)

            def hidden0(m, m0, c):
                slot, t = m0 // 4 % 2, m0 % 4
                w = slice(128 * c, 128 * c + 128)
                if m0 >= 1:
                    pe.wait_ge(s["act"], 2 * (4 * m - 3 + c))
                three(PS[:, c, :], WH[:, slot, w], WL[:, slot, w], blk(HH, t), blk(HL, t), True, True)\
                    .then_inc(s["h"], 1)

            def output0(m, m0, c):
                slot = m0 // 4 % 2
                w = slice(512 + 128 * c, 640 + 128 * c)
                pe.wait_ge(s["lo"], 4 * m + c + 1)
                if c == 0 and m0 >= 4:
                    pe.wait_ge(s["ymul"], m - 3)
                elif c == 0 and m0 >= 2:
                    pe.wait_ge(s["acc_init"], 1 + m0)
                mm = three(PS[:, 4 + m0 % 4, :], WH[:, slot, w], WL[:, slot, w], GH[:, m0 % 2, c, :],
                           GL[:, m0 % 2, c, :], c == 0, c == 3)
                if c == 3:
                    mm.then_inc(s["y"], 1)

            def step0(m, m0, e_next, ahead=True, between=None):
                if ahead and m0 % 4 == 3:
                    pe.wait_ge(s["split"], 2 * e_next + 2)
                for c in range(4):
                    if ahead:
                        hidden0(m + 1, m0 + 1, c)
                    output0(m, m0, c)
                    if between:
                        between(c)

            def routes_between(c):
                if c == 1 or c == 2:
                    route_out(0, E0, 2 * c - 2)
                    route_out(0, E0, 2 * c - 1)

            def biases_between(c):
                bias_out(c)

            pe.wait_ge(hl_done, 4)
            pe.wait_ge(s["split"], 2)
            for c in range(4):
                hidden0(0, 0, c)
            step0(0, 0, 1, between=routes_between)
            step0(1, 1, 1, between=biases_between)
            for m in range(2, 8):
                step0(m, m, m // 4 + 1)
            with pe.Fori(1, 4) as it:
                for u in range(8):
                    step0(8 * it + u, 8 + u, 2 * it + u // 4 + 1)
            for m in range(32, 35):
                step0(m, m, 8)

            def between_last(c):
                if c == 1:
                    mean(2, 0)
                elif c == 2:
                    mean(2, 1)

            step0(35, 35, 8, ahead=False, between=between_last)
            variance(2, 0)
            variance(2, 1)
            mean(2, 2)
            mean(2, 3)
            variance(3, 0)

            def projections(first, end):
                for i in range(first, end):
                    p, t = projected[i]
                    w = slice(128 * p, 128 * p + 128)
                    pe.wait_ge(hl_done, 4 + t + 1)
                    if i >= 8:
                        pe.wait_ge(p1_done, evacuated(i - 8))
                        if projected[i - 8][0] == 3:
                            pe.wait_ge(hsi_done, projected[i - 8][1] + 1)
                    three(PS[:, i % 8, :], LH[:, w], LL[:, w], blk(HH, t), blk(HL, t), True, True)\
                        .then_inc(p1_psum, 1)

            for k, t in turns[3:7]:
                variance(k, t)
            pe.wait_ge(l1_split, 2)
            projections(0, 3)
            variance(3, 3)
            projections(3, 4)
            pe.wait_ge(lnv_done, 16)
            projections(4, 16)
            pe.wait_ge(p1_done, 12)
            pe.wait_ge(hsi_done, 4)
            for t in range(3):
                variance(4, t)

            def mlp_hidden(t):
                for c in range(3):
                    i = 3 * t + c
                    pe.wait_ge(hl_done, 8 + t + 1)
                    if t >= 1:
                        pe.wait_ge(pf_done, i - 2)
                    for which in range(2):
                        w = slice(512 + 384 * which + 128 * c, 640 + 384 * which + 128 * c)
                        mm = three(PS[:, 3 * which + c, :], LH[:, w], LL[:, w], blk(HH, t), blk(HL, t), True, True)
                    mm.then_inc(mlp_psum, 1)
                    if t == 0 and c == 0:
                        variance(4, 3)

            def mlp_output(t):
                if t >= 2:
                    pe.wait_ge(z_done, t - 1)
                else:
                    pe.wait_ge(lnv_done, 20)
                for c in range(3):
                    pe.wait_ge(pl_done, 3 * t + c + 1)
                    w = slice(1280 + 128 * c, 1408 + 128 * c)
                    mm = three(PS[:, 6 + t % 2, :], LH[:, w], LL[:, w], GH[:, t % 2, c, :], GL[:, t % 2, c, :],
                               c == 0, c == 2)
                mm.then_inc(z_psum, 1)

            mlp_hidden(0)
            for t in range(3):
                mlp_hidden(t + 1)
                mlp_output(t)

            pe.wait_ge(pf_done, 12)
            mean(5, 0)
            mean(5, 1)
            mlp_output(3)
            mean(5, 2)
            variance(5, 0)
            variance(5, 1)
            mean(5, 3)
            variance(5, 2)
            router(1, 0)
            variance(5, 3)
            router(1, 1)
            router(1, 2)
            router(1, 3)
            s1 = moe[1]

            def hidden1(m, m0, c):
                slot, t = m0 // 4 % 2, m0 % 4
                if m0 >= 1:
                    pe.wait_ge(s1["act"], 2 * m - 1 + c)
                    pe.wait_ge(s1["prod"], 2 * m - 1 + c)
                for which in range(2):
                    w = slice(256 * which + 128 * c, 256 * which + 128 * c + 128)
                    mm = three(PS[:, 2 * which + c, :], WH[:, slot, w], WL[:, slot, w], blk(HH, t), blk(HL, t),
                               True, True)
                mm.then_inc(s1["h"], 1)

            def output1(m, m0, c):
                slot = m0 // 4 % 2
                w = slice(512 + 128 * c, 640 + 128 * c)
                pe.wait_ge(s1["lo"], 2 * m + c + 1)
                if c == 0 and m0 >= 4:
                    pe.wait_ge(s1["ymul"], m - 3)
                elif c == 0 and m0 >= 2:
                    pe.wait_ge(s1["ct"], 1 + m0)
                mm = three(PS[:, 4 + m0 % 4, :], WH[:, slot, w], WL[:, slot, w], GH[:, m0 % 2, c, :],
                           GL[:, m0 % 2, c, :], c == 0, c == 1)
                if c == 1:
                    mm.then_inc(s1["y"], 1)

            def step1(m, m0, e_next, ahead=True):
                if ahead and m0 % 4 == 3:
                    pe.wait_ge(s1["split"], 2 * e_next + 2)
                for c in range(2):
                    if ahead:
                        hidden1(m + 1, m0 + 1, c)
                    output1(m, m0, c)

            pe.wait_ge(hl_done, 16)
            pe.wait_ge(s1["split"], 2)
            for c in range(2):
                hidden1(0, 0, c)
            for t in range(NBLK):
                route_out(1, E1, t)
            for m in range(8):
                step1(m, m, m // 4 + 1)
            with pe.Fori(1, 3) as it:
                for u in range(8):
                    step1(8 * it + u, 8 + u, 2 * it + u // 4 + 1)
            for m in range(24, 32):
                step1(m, m, m // 4 + 1, ahead=m < 31)


def layouts(inputs):
    import numpy as np

    a = {k: np.asarray(v) for k, v in inputs.items()}
    f4 = np.float32

    def heads(v, parts):
        v = v.reshape(v.shape[:-1] + (4, 4, 1, 8))
        out = np.zeros(v.shape[:-2] + (4, 8), f4)
        out[..., :parts, :] = v
        return out.reshape(out.shape[:-4] + (4, 128))

    vecs = np.zeros((128, VN), f4)

    def put(name, v):
        v = v.reshape(v.shape[0], -1)
        vecs[:v.shape[0], VAT[name]:VAT[name] + v.shape[1]] = v

    bk = heads(a["L0_attn_bku"][:128], 3)
    for j in range(4):
        bk[:, 32 * j + 24:32 * j + 26] = 1.0
    row = np.arange(128) % 32 // 8
    b1 = np.concatenate([a["L0_ffn_spec_b1"], a["L0_ffn_shared_b1"][None]])
    put("bo", a["L0_attn_bo"])
    put("bq", heads(a["L0_attn_bq"], 3).T)
    put("bk", bk.T)
    put("q_sign", np.array([1, -1, 1, 1], f4)[row])
    put("q_keep", np.array([0, 1, 0, 0], f4)[row])
    put("k_sign", np.array([1, 1, -1, 1], f4)[row])
    put("k_keep", np.array([0, 0, 1, 0], f4)[row])
    put("b1", b1.reshape(E0, 4, 128).transpose(2, 0, 1))
    put("pb", np.stack([a[f"L1_attn_fc_{n}"] for n in ("r_b", "i_b", "gate_b", "b")], 1))
    put("gb", a["L1_attn_mlp_gate_b"].reshape(3, 128).T)
    put("fb", a["L1_attn_mlp_fc_b"].reshape(3, 128).T)
    put("outb", a["L1_attn_out_b"])
    put("alpha", a["L1_attn_alpha"].reshape(128))
    put("norm", a["L1_attn_norm_w"])
    put("norm2", a["L1_attn_norm2_w"])
    put("bkd", a["L0_attn_bkd"])
    put("c", np.concatenate([a["L0_c"], a["L1_c"]]).T)
    put("prio", np.tile(np.arange(8, 0, -1, dtype=f4), (128, 1)))

    wo = np.zeros((128, 4, 128), f4)
    for j in range(4):
        rows = a["L0_attn_Wo"].reshape(4, 4, 8, 128)[:, j].transpose(1, 0, 2)
        wo[32 * j:32 * j + 16] = np.concatenate([rows, rows])
    l1 = [a[f"L1_attn_fc_{n}"].T for n in ("r_w", "i_w", "gate_w", "w")]
    l1 += [a["L1_attn_mlp_gate_w"].T, a["L1_attn_mlp_fc_w"].T,
           a["L1_attn_out_w"].T.reshape(3, 128, 128).transpose(1, 0, 2).reshape(128, 384)]
    mats = np.concatenate([a["L0_attn_Wkd"], heads(a["L0_attn_Wq"], 3).reshape(128, 512), wo.reshape(128, 512),
                           a["L0_ffn_router_w"].T, a["L1_ffn_Wg"]] + l1, 1)
    wk = np.concatenate([heads(a["L0_attn_Wku"][:, :128], 3).reshape(32, 512), a["L0_attn_Wku"][:, 128:]], 1)
    rows = np.concatenate([a["L0_attn_bku"][128:], a["L0_ffn_router_b"]])
    up = np.concatenate([a["L0_ffn_spec_w1"], a["L0_ffn_shared_w1"][None]]).transpose(0, 2, 1)
    down = np.concatenate([a["L0_ffn_spec_w2"], a["L0_ffn_shared_w2"][None]]).transpose(0, 2, 1)
    down = down.reshape(E0, 4, 128, 128).transpose(0, 2, 1, 3).reshape(E0, 128, 512)
    down1 = a["L1_ffn_W2"].reshape(E1, 2, 128, 128).transpose(0, 2, 1, 3).reshape(E1, 128, 256)
    return dict(
        xT=a["L0_attn_x"].reshape(TOK, D).T,
        wmod=np.concatenate([a["L0_wmod"], a["L1_wmod"]], 1),
        vecs=vecs,
        mats=mats,
        kmats=np.concatenate([wk, wk]),
        rows=np.tile(rows, (128, 1)),
        b2=np.concatenate([a["L0_ffn_spec_b2"], a["L0_ffn_shared_b2"][None]]),
        w0=np.concatenate([up, down], 2),
        w1=np.concatenate([a["L1_ffn_W1"], a["L1_ffn_W3"], down1], 2),
    )


def kernel(**inputs):
    import numpy as np
    import concourse.bacc as bacc
    from concourse.bass_utils import run_bass_kernel_spmd

    nc = bacc.Bacc("TRN2", target_bir_lowering=False, num_devices=1)
    arrays, args = {}, []
    for name, value in layouts(inputs).items():
        value = np.ascontiguousarray(value)
        arrays[f"in_{name}"] = value
        args.append(nc.dram_tensor(f"in_{name}", value.shape, mybir.dt.from_np(value.dtype),
                                   kind="ExternalInput").ap())
    for n, ne in enumerate((E0, E1)):
        args.append(nc.dram_tensor(f"comb_{n}", (ne, TOK), mybir.dt.float32, kind="Internal").ap())
    args.append(nc.dram_tensor("out_xT", (D, TOK), mybir.dt.float32, kind="ExternalOutput").ap())
    build(nc, *args)
    r = run_bass_kernel_spmd(nc, [arrays], core_ids=[0])
    return np.ascontiguousarray(r.results[0]["out_xT"].T).reshape(BATCHES, SEQ, D)
```
